# Optimizing a Trainium2 kernel written in Bass

```python
import numpy as np
import jax
import jax.numpy as jnp

def _softmax(x, axis=-1):
    return jax.nn.softmax(x, axis=axis)

def _gelu(x):
    return jax.nn.gelu(x, approximate=True)

def _silu(x):
    return jax.nn.silu(x)

def _sigmoid(x):
    return jax.nn.sigmoid(x)

def _layernorm(x, axis=-1, eps=1e-05):
    m = jnp.mean(x, axis=axis, keepdims=True)
    v = jnp.var(x, axis=axis, keepdims=True)
    return (x - m) / jnp.sqrt(v + eps)

def _scatter_add(tgt, idx, src, axis=0):
    return tgt.at[idx].add(src)

def _segment_sum(src, seg, n):
    return jax.ops.segment_sum(src, seg, n)
kernel_name = 'mk_dlrm_tower_d1_rec_r8_594f99'

def setup_inputs(seed: int=0):
    np.random.seed(seed)
    _w = jnp.asarray

    def _rec_inputs():
        import jax
        import jax.numpy as jnp
        _tk = jax.random.key(seed)
        dense_ctx = jax.random.normal(jax.random.fold_in(_tk, 190), (1024, 16), jnp.float32)
        ids = jnp.stack([jax.random.randint(jax.random.fold_in(_tk, 200 + f), (1024,), 0, v, jnp.int32) for f, v in enumerate([125000, 125000, 1000, 1250, 125000, 1250, 12500, 1000, 125000, 12500, 125000, 1250, 1250, 125000, 1000, 12500, 1000, 12500, 12500, 1000, 1000, 125000, 12500, 125000, 12500, 125000, 1000, 125000, 1250, 12500, 12500, 1000, 1000, 12500, 1250, 125000, 1250, 12500, 1250])], axis=1)
        tbl_0 = 0.05 * jax.random.normal(jax.random.fold_in(_tk, 500 + 0), (125000, 16), jnp.float32)
        tbl_1 = 0.05 * jax.random.normal(jax.random.fold_in(_tk, 500 + 1), (125000, 16), jnp.float32)
        tbl_2 = 0.05 * jax.random.normal(jax.random.fold_in(_tk, 500 + 2), (1000, 16), jnp.float32)
        tbl_3 = 0.05 * jax.random.normal(jax.random.fold_in(_tk, 500 + 3), (1250, 16), jnp.float32)
        tbl_4 = 0.05 * jax.random.normal(jax.random.fold_in(_tk, 500 + 4), (125000, 16), jnp.float32)
        tbl_5 = 0.05 * jax.random.normal(jax.random.fold_in(_tk, 500 + 5), (1250, 16), jnp.float32)
        tbl_6 = 0.05 * jax.random.normal(jax.random.fold_in(_tk, 500 + 6), (12500, 16), jnp.float32)
        tbl_7 = 0.05 * jax.random.normal(jax.random.fold_in(_tk, 500 + 7), (1000, 16), jnp.float32)
        tbl_8 = 0.05 * jax.random.normal(jax.random.fold_in(_tk, 500 + 8), (125000, 16), jnp.float32)
        tbl_9 = 0.05 * jax.random.normal(jax.random.fold_in(_tk, 500 + 9), (12500, 16), jnp.float32)
        tbl_10 = 0.05 * jax.random.normal(jax.random.fold_in(_tk, 500 + 10), (125000, 16), jnp.float32)
        tbl_11 = 0.05 * jax.random.normal(jax.random.fold_in(_tk, 500 + 11), (1250, 16), jnp.float32)
        tbl_12 = 0.05 * jax.random.normal(jax.random.fold_in(_tk, 500 + 12), (1250, 16), jnp.float32)
        tbl_13 = 0.05 * jax.random.normal(jax.random.fold_in(_tk, 500 + 13), (125000, 16), jnp.float32)
        tbl_14 = 0.05 * jax.random.normal(jax.random.fold_in(_tk, 500 + 14), (1000, 16), jnp.float32)
        tbl_15 = 0.05 * jax.random.normal(jax.random.fold_in(_tk, 500 + 15), (12500, 16), jnp.float32)
        tbl_16 = 0.05 * jax.random.normal(jax.random.fold_in(_tk, 500 + 16), (1000, 16), jnp.float32)
        tbl_17 = 0.05 * jax.random.normal(jax.random.fold_in(_tk, 500 + 17), (12500, 16), jnp.float32)
        tbl_18 = 0.05 * jax.random.normal(jax.random.fold_in(_tk, 500 + 18), (12500, 16), jnp.float32)
        tbl_19 = 0.05 * jax.random.normal(jax.random.fold_in(_tk, 500 + 19), (1000, 16), jnp.float32)
        tbl_20 = 0.05 * jax.random.normal(jax.random.fold_in(_tk, 500 + 20), (1000, 16), jnp.float32)
        tbl_21 = 0.05 * jax.random.normal(jax.random.fold_in(_tk, 500 + 21), (125000, 16), jnp.float32)
        tbl_22 = 0.05 * jax.random.normal(jax.random.fold_in(_tk, 500 + 22), (12500, 16), jnp.float32)
        tbl_23 = 0.05 * jax.random.normal(jax.random.fold_in(_tk, 500 + 23), (125000, 16), jnp.float32)
        tbl_24 = 0.05 * jax.random.normal(jax.random.fold_in(_tk, 500 + 24), (12500, 16), jnp.float32)
        tbl_25 = 0.05 * jax.random.normal(jax.random.fold_in(_tk, 500 + 25), (125000, 16), jnp.float32)
        tbl_26 = 0.05 * jax.random.normal(jax.random.fold_in(_tk, 500 + 26), (1000, 16), jnp.float32)
        tbl_27 = 0.05 * jax.random.normal(jax.random.fold_in(_tk, 500 + 27), (125000, 16), jnp.float32)
        tbl_28 = 0.05 * jax.random.normal(jax.random.fold_in(_tk, 500 + 28), (1250, 16), jnp.float32)
        tbl_29 = 0.05 * jax.random.normal(jax.random.fold_in(_tk, 500 + 29), (12500, 16), jnp.float32)
        tbl_30 = 0.05 * jax.random.normal(jax.random.fold_in(_tk, 500 + 30), (12500, 16), jnp.float32)
        tbl_31 = 0.05 * jax.random.normal(jax.random.fold_in(_tk, 500 + 31), (1000, 16), jnp.float32)
        tbl_32 = 0.05 * jax.random.normal(jax.random.fold_in(_tk, 500 + 32), (1000, 16), jnp.float32)
        tbl_33 = 0.05 * jax.random.normal(jax.random.fold_in(_tk, 500 + 33), (12500, 16), jnp.float32)
        tbl_34 = 0.05 * jax.random.normal(jax.random.fold_in(_tk, 500 + 34), (1250, 16), jnp.float32)
        tbl_35 = 0.05 * jax.random.normal(jax.random.fold_in(_tk, 500 + 35), (125000, 16), jnp.float32)
        tbl_36 = 0.05 * jax.random.normal(jax.random.fold_in(_tk, 500 + 36), (1250, 16), jnp.float32)
        tbl_37 = 0.05 * jax.random.normal(jax.random.fold_in(_tk, 500 + 37), (12500, 16), jnp.float32)
        tbl_38 = 0.05 * jax.random.normal(jax.random.fold_in(_tk, 500 + 38), (1250, 16), jnp.float32)
        _rk = jax.random.fold_in(_tk, 7)
        W_top1 = 0.0606339 * jax.random.normal(jax.random.fold_in(_tk, 801), (272, 512), jnp.float32)
        W_top2 = 0.0441942 * jax.random.normal(jax.random.fold_in(_tk, 802), (512, 256), jnp.float32)
        W_top3 = 0.0625 * jax.random.normal(jax.random.fold_in(_tk, 803), (256, 1), jnp.float32)
        b_top1 = jnp.zeros((512,), jnp.float32)
        b_top2 = jnp.zeros((256,), jnp.float32)
        return (dense_ctx, ids, tbl_0, tbl_1, tbl_2, tbl_3, tbl_4, tbl_5, tbl_6, tbl_7, tbl_8, tbl_9, tbl_10, tbl_11, tbl_12, tbl_13, tbl_14, tbl_15, tbl_16, tbl_17, tbl_18, tbl_19, tbl_20, tbl_21, tbl_22, tbl_23, tbl_24, tbl_25, tbl_26, tbl_27, tbl_28, tbl_29, tbl_30, tbl_31, tbl_32, tbl_33, tbl_34, tbl_35, tbl_36, tbl_37, tbl_38, W_top1, b_top1, W_top2, b_top2, W_top3)
    dense_ctx, ids, tbl_0, tbl_1, tbl_2, tbl_3, tbl_4, tbl_5, tbl_6, tbl_7, tbl_8, tbl_9, tbl_10, tbl_11, tbl_12, tbl_13, tbl_14, tbl_15, tbl_16, tbl_17, tbl_18, tbl_19, tbl_20, tbl_21, tbl_22, tbl_23, tbl_24, tbl_25, tbl_26, tbl_27, tbl_28, tbl_29, tbl_30, tbl_31, tbl_32, tbl_33, tbl_34, tbl_35, tbl_36, tbl_37, tbl_38, W_top1, b_top1, W_top2, b_top2, W_top3 = _rec_inputs()

    def _L0_rec_setup():
        import jax, jax.numpy as jnp
        import numpy as np
        NUM_FIELD = 39
        CIN_SIZE = [128, 128]
        EMBED_DIM = 16
        BATCH = 256
        key = jax.random.key(seed)
        k1, k2, k3 = jax.random.split(key, 3)
        x_emb = jax.random.normal(k1, (BATCH, NUM_FIELD, EMBED_DIM), dtype=jnp.float32)
        W0 = jax.random.normal(k2, (CIN_SIZE[0], NUM_FIELD * NUM_FIELD), dtype=jnp.float32) * 0.02
        W1 = jax.random.normal(k3, (CIN_SIZE[1], CIN_SIZE[0] * NUM_FIELD), dtype=jnp.float32) * 0.02
        return {'x_emb': x_emb, 'W0': W0, 'W1': W1}
    _L0_rec_all = _L0_rec_setup()
    _L0_rec_in = {k: v for k, v in _L0_rec_all.items() if k in ('W0', 'W1')}
    del _L0_rec_all
    return {'dense_ctx': dense_ctx, 'ids': ids, 'tbl_0': tbl_0, 'tbl_1': tbl_1, 'tbl_2': tbl_2, 'tbl_3': tbl_3, 'tbl_4': tbl_4, 'tbl_5': tbl_5, 'tbl_6': tbl_6, 'tbl_7': tbl_7, 'tbl_8': tbl_8, 'tbl_9': tbl_9, 'tbl_10': tbl_10, 'tbl_11': tbl_11, 'tbl_12': tbl_12, 'tbl_13': tbl_13, 'tbl_14': tbl_14, 'tbl_15': tbl_15, 'tbl_16': tbl_16, 'tbl_17': tbl_17, 'tbl_18': tbl_18, 'tbl_19': tbl_19, 'tbl_20': tbl_20, 'tbl_21': tbl_21, 'tbl_22': tbl_22, 'tbl_23': tbl_23, 'tbl_24': tbl_24, 'tbl_25': tbl_25, 'tbl_26': tbl_26, 'tbl_27': tbl_27, 'tbl_28': tbl_28, 'tbl_29': tbl_29, 'tbl_30': tbl_30, 'tbl_31': tbl_31, 'tbl_32': tbl_32, 'tbl_33': tbl_33, 'tbl_34': tbl_34, 'tbl_35': tbl_35, 'tbl_36': tbl_36, 'tbl_37': tbl_37, 'tbl_38': tbl_38, 'W_top1': W_top1, 'b_top1': b_top1, 'W_top2': W_top2, 'b_top2': b_top2, 'W_top3': W_top3, 'L0_rec_W0': _L0_rec_in['W0'], 'L0_rec_W1': _L0_rec_in['W1']}

def reference(dense_ctx, ids, tbl_0, tbl_1, tbl_2, tbl_3, tbl_4, tbl_5, tbl_6, tbl_7, tbl_8, tbl_9, tbl_10, tbl_11, tbl_12, tbl_13, tbl_14, tbl_15, tbl_16, tbl_17, tbl_18, tbl_19, tbl_20, tbl_21, tbl_22, tbl_23, tbl_24, tbl_25, tbl_26, tbl_27, tbl_28, tbl_29, tbl_30, tbl_31, tbl_32, tbl_33, tbl_34, tbl_35, tbl_36, tbl_37, tbl_38, W_top1, b_top1, W_top2, b_top2, W_top3, L0_rec_W0, L0_rec_W1):
    import jax
    import jax.numpy as jnp

    def _L0_rec_ref(x_emb, W0, W1):
        import jax, jax.numpy as jnp
        import numpy as np
        NUM_FIELD = 39
        CIN_SIZE = [128, 128]
        EMBED_DIM = 16
        BATCH = 256
        B, F, D = x_emb.shape
        x = x_emb
        outs = []
        for W in (W0, W1):
            last = x.shape[1]
            inter = (x[:, :, None, :] * x_emb[:, None, :, :]).reshape(B, last * F, D)
            x = jnp.einsum('bid,hi->bhd', inter, W)
            outs.append(x.sum(axis=-1))
        return jnp.concatenate(outs, axis=-1)
    e = jnp.stack([tbl_0[ids[:, 0]], tbl_1[ids[:, 1]], tbl_2[ids[:, 2]], tbl_3[ids[:, 3]], tbl_4[ids[:, 4]], tbl_5[ids[:, 5]], tbl_6[ids[:, 6]], tbl_7[ids[:, 7]], tbl_8[ids[:, 8]], tbl_9[ids[:, 9]], tbl_10[ids[:, 10]], tbl_11[ids[:, 11]], tbl_12[ids[:, 12]], tbl_13[ids[:, 13]], tbl_14[ids[:, 14]], tbl_15[ids[:, 15]], tbl_16[ids[:, 16]], tbl_17[ids[:, 17]], tbl_18[ids[:, 18]], tbl_19[ids[:, 19]], tbl_20[ids[:, 20]], tbl_21[ids[:, 21]], tbl_22[ids[:, 22]], tbl_23[ids[:, 23]], tbl_24[ids[:, 24]], tbl_25[ids[:, 25]], tbl_26[ids[:, 26]], tbl_27[ids[:, 27]], tbl_28[ids[:, 28]], tbl_29[ids[:, 29]], tbl_30[ids[:, 30]], tbl_31[ids[:, 31]], tbl_32[ids[:, 32]], tbl_33[ids[:, 33]], tbl_34[ids[:, 34]], tbl_35[ids[:, 35]], tbl_36[ids[:, 36]], tbl_37[ids[:, 37]], tbl_38[ids[:, 38]]], axis=1)
    z = _L0_rec_ref(e, L0_rec_W0, L0_rec_W1)
    z = z.reshape(z.shape[0], -1)
    h = jnp.concatenate([z, dense_ctx], axis=1)
    h = jnp.maximum(h @ W_top1 + b_top1, 0.0)
    h = jnp.maximum(h @ W_top2 + b_top2, 0.0)
    y = h @ W_top3
    return y

_drawn_inputs = setup_inputs


def setup_inputs(seed=0):
    import zlib

    import numpy as np

    out = dict(_drawn_inputs(seed))
    spreads = {'b_top1': (0.0, 0.1), 'b_top2': (0.0, 0.1)}
    factors = {'tbl_0': 8.0,
     'tbl_1': 8.0,
     'tbl_2': 8.0,
     'tbl_3': 8.0,
     'tbl_4': 8.0,
     'tbl_5': 8.0,
     'tbl_6': 8.0,
     'tbl_7': 8.0,
     'tbl_8': 8.0,
     'tbl_9': 8.0,
     'tbl_10': 8.0,
     'tbl_11': 8.0,
     'tbl_12': 8.0,
     'tbl_13': 8.0,
     'tbl_14': 8.0,
     'tbl_15': 8.0,
     'tbl_16': 8.0,
     'tbl_17': 8.0,
     'tbl_18': 8.0,
     'tbl_19': 8.0,
     'tbl_20': 8.0,
     'tbl_21': 8.0,
     'tbl_22': 8.0,
     'tbl_23': 8.0,
     'tbl_24': 8.0,
     'tbl_25': 8.0,
     'tbl_26': 8.0,
     'tbl_27': 8.0,
     'tbl_28': 8.0,
     'tbl_29': 8.0,
     'tbl_30': 8.0,
     'tbl_31': 8.0,
     'tbl_32': 8.0,
     'tbl_33': 8.0,
     'tbl_34': 8.0,
     'tbl_35': 8.0,
     'tbl_36': 8.0,
     'tbl_37': 8.0,
     'tbl_38': 8.0,
     'L0_rec_W1': 8.0}
    for name, (base, spread) in spreads.items():
        noise = np.random.default_rng([zlib.crc32(name.encode()), seed]).standard_normal(out[name].shape)
        drawn = base * np.exp(spread * noise) if base else spread * noise
        out[name] = jnp.asarray(drawn.astype(out[name].dtype))
    for name, factor in factors.items():
        out[name] = (out[name] * factor).astype(out[name].dtype)
    return out
```

```python
from contextlib import ExitStack

import concourse.bass as bass
import numpy as np
from concourse import mybir

F32 = mybir.dt.float32
BF16 = mybir.dt.bfloat16
I32 = mybir.dt.int32
ALU = mybir.AluOpType
ACT = mybir.ActivationFunctionType

B, FIELDS, D, H = 1024, 39, 16, 128
HID1, HID2 = 512, 256
P = 128
TILES = B // P
PAIRS = TILES // 2
ROWS = 2 * P
SHIFTS = 3
CH = SHIFTS * FIELDS
NCH = -(-(FIELDS // 2 + 1) // SHIFTS)
BLK = 32
COLS = BLK * D
STEPS = ROWS // BLK
GRP = P // D
GROUPS = BLK // GRP
FE = FIELDS + 1
PROD = NCH * STEPS
SLOTS = NCH + 1
ECOL = 4
V_USES = SLOTS * STEPS
NV_BANKS, NS_BANKS, NPROD, LEAD = 4, 3, 8, 3
HALF = D // 2
A_AT, E_AT = NCH * CH, (NCH + 1) * CH
KT1, MT1 = 3, HID1 // P
MT2 = HID2 // P


def chunk(pos):
    return pos - (pos > ECOL)


def scalar_uses(m, start_next):
    turn = m % 4 == 3 and start_next
    return ([("x1t", m), ("g0", m), ("g1", m), ("g2", m), ("g3", m)] + [("turn0", m), ("turn1", m)] * turn
            + [("z2", m)] * (m % STEPS == 0) + [("opa", m)] * start_next
            + [("h1a", m), ("h1b", m), ("h2", m), ("y", m)] * (m % STEPS == 0))


FIRST = [("turn0", 0), ("turn1", 0), ("opa", -1), ("opa", 0)]
BODY = [u for m in [*range(1, STEPS), 0] for u in scalar_uses(m, True)]
LAST = [u for m in range(1, STEPS) for u in scalar_uses(m, m < STEPS - 1)] + scalar_uses(STEPS, False)
S_USES = len(BODY)
assert PROD % NPROD == 0 and S_USES % NS_BANKS == 0 and V_USES % NV_BANKS == 0


class Phase:

    def __init__(self, j, order, before):
        self.j, self.order, self.before = j, order, before

    def count(self, use):
        return self.j * S_USES + (self.before + self.order.index(use) + 1)

    def bank(self, use):
        return (self.before + self.order.index(use)) % NS_BANKS


def phases(eng, opening, step):
    first = Phase(0, FIRST, 0)
    opening(first)
    step(first, 0, 0)
    with eng.Fori(0, PAIRS - 1) as j:
        body = Phase(j, BODY, len(FIRST))
        for m in range(1, STEPS):
            step(body, j, m)
        step(body, j + 1, 0)
    last = Phase(PAIRS - 1, LAST, len(FIRST))
    for m in range(1, STEPS + 1):
        step(last, PAIRS - 1, m)


def cin_tower(nc, ids, tables, dense_t, w0_ij, w0_ji, w1_t, w_top1, w_top2, w_top3, b_top1, b_top2,
              pick, ident_bf, ident_f, own_rows, out):
    with ExitStack() as ctx:
        def sb(name, shape, dt=F32):
            return ctx.enter_context(nc.sbuf_tensor(name, shape, dt))

        def sem(name):
            return ctx.enter_context(nc.semaphore(name))

        pick_sb = sb("pick_sb", [CH, (NCH + 1) * CH + FE], BF16)
        idb = sb("idb", [P, P], BF16)
        idf = sb("idf", [P, P])
        own = sb("own", [P, GRP])
        w0a = sb("w0a", [CH, NCH, H])
        w0b = sb("w0b", [CH, NCH, H])
        w0s = sb("w0s", [CH, NCH, H])
        w1_sb = sb("w1_sb", [H, FIELDS, H])
        wt1 = sb("wt1", [P, KT1, HID1])
        wt2 = sb("wt2", [P, MT1, HID2])
        wt3 = sb("wt3", [P, MT2, P])
        bt1 = sb("bt1", [P, MT1])
        bt2 = sb("bt2", [P, MT2])
        dense_sb = sb("dense_sb", [P, B])
        idx = [sb(f"idx{t}", [P, FIELDS], I32) for t in range(2)]
        emb = [sb(f"emb{t}", [P, FIELDS, D]) for t in range(2)]
        rest = sb("rest", [P, FIELDS, D])
        parts = sb("parts", [P, D, 3, FIELDS], BF16)
        emb_t = [sb(f"emb_t{t}", [CH, P, D], BF16) for t in range(2)]
        opa = [sb(f"opa{i}", [CH, COLS]) for i in range(2)]
        prod = [sb(f"prod{i}", [CH, COLS]) for i in range(NPROD)]
        x1 = [sb(f"x1_{i}", [H, COLS]) for i in range(2)]
        x1t = [sb(f"x1t{i}", [P, GROUPS, H]) for i in range(2)]
        ediag = [sb(f"ediag{i}", [P, GROUPS, GRP, FE]) for i in range(2)]
        g_sb = sb("g_sb", [H, FE, ROWS])
        z2 = sb("z2", [H, ROWS])
        h1 = sb("h1", [P, MT1, ROWS])
        h2 = sb("h2", [P, MT2, ROWS])
        y = sb("y", [1, B])

        v_ps = [ctx.enter_context(nc.psum_tensor(f"v_ps{i}", [P, 512], F32)) for i in range(NV_BANKS)]
        s_ps = [ctx.enter_context(nc.psum_tensor(f"s_ps{i}", [P, 512], F32)) for i in range(NS_BANKS)]
        x1_ps = ctx.enter_context(nc.psum_tensor("x1_ps", [P, 512], F32))

        loads = sem("loads")
        idx_ready = [sem(f"idx_ready{t}") for t in range(2)]
        gathered = [sem(f"gathered{t}") for t in range(2)]
        tile_begun = sem("tile_begun")
        rest_ready = sem("rest_ready")
        part0_ready = sem("part0_ready")
        part1_ready = sem("part1_ready")
        part2_ready = sem("part2_ready")
        w0_ready = sem("w0_ready")
        pads_ready = sem("pads_ready")
        s_full = sem("s_full")
        s_drained = sem("s_drained")
        v_full = sem("v_full")
        v_drained = sem("v_drained")
        prod_free = sem("prod_free")
        x1_ready = sem("x1_ready")
        y_stored = sem("y_stored")

        LOADS = [(pick_sb[:, :], pick.bitcast(BF16)), (idb[:, :], ident_bf.bitcast(BF16)), (w0a[:, :, :], w0_ij), (w0b[:, :, :], w0_ji),
                 (idf[:, :], ident_f), (own[:, :], own_rows), (w1_sb[:, :, :], w1_t),
                 (wt1[:, 0:2, :], w_top1[0:2 * P].rearrange("(k p) n -> p k n", p=P)),
                 (wt1[0:D, 2, :], w_top1[2 * P:2 * P + D]),
                 (wt2[:, :, :], w_top2.rearrange("(k p) n -> p k n", p=P)),
                 (wt3[:, :, :], w_top3.rearrange("(k p) n -> p k n", p=P)),
                 (bt1[:, :], b_top1), (bt2[:, :], b_top2), (dense_sb[0:D, :], dense_t)]

        block = ctx.enter_context(nc.Block())

        @block.sync
        def _(sp):
            def load_idx(j, t):
                if not isinstance(j, int):
                    sp.wait_ge(gathered[t], j * (16 * FIELDS))
                sp.dma_start(idx[t][:, :], ids[bass.ds(j * 2 + t, 1)].rearrange("a p f -> (a p) f")
                             ).then_inc(idx_ready[t], 16)

            for t in range(2):
                load_idx(0, t)
            for n, (dst, src) in enumerate(LOADS):
                if n == 7:
                    sp.wait_ge(pads_ready, 2)
                sp.dma_start(dst, src).then_inc(loads, 16)
            with sp.Fori(1, PAIRS) as j:
                for t in range(2):
                    load_idx(j, t)
            sp.wait_ge(s_drained, Phase(PAIRS - 1, LAST, len(FIRST)).count(("y", STEPS)) + NS_BANKS)
            sp.dma_start(out, y[0:1, :]).then_inc(y_stored, 16)
            sp.wait_ge(y_stored, 16)

        @block.gpsimd
        def _(pool):
            with pool.Fori(0, PAIRS) as j:
                for t in range(2):
                    pool.wait_ge(idx_ready[t], j * 16 + 16)
                    pool.wait_ge(rest_ready, j * 2 + (t + 1))
                    pool.sem_inc(tile_begun, 1)
                    for f in range(FIELDS):
                        nc.gpsimd.indirect_dma_start(emb[t][:, f, :], None, tables[f],
                                                     bass.IndirectOffsetOnAxis(idx[t][:, f:f + 1], 0)
                                                     ).then_inc(gathered[t], 16)

        @block.tensor
        def _(pe):
            def s_bank(ph, use):
                pe.wait_ge(s_drained, ph.count(use))
                return s_ps[ph.bank(use)]

            def await_drained(ph, use):
                pe.wait_ge(s_drained, ph.count(use) + NS_BANKS)

            def await_slot(jb, u, extra=0):
                pe.wait_ge(v_drained, jb * V_USES + (u + 1 + extra))

            def turn(ph, m, half):
                bank = s_bank(ph, (f"turn{half}", m))
                view = bank[:, :].bitcast(BF16)
                for d in range(HALF):
                    mm = nc.tensor.transpose(view[0:CH, d * P:(d + 1) * P],
                                             parts[:, half * HALF + d, :, :].rearrange("p a f -> p (a f)"), idb[:, :])
                mm.then_inc(s_full, 1)

            def turns_ready(tile):
                for part in (part0_ready, part1_ready, part2_ready):
                    pe.wait_ge(part, tile + 1)

            def spread_a(ph, m_step, m):
                nc.tensor.matmul(s_bank(ph, ("opa", m_step))[0:CH, :], pick_sb[:, A_AT:A_AT + CH], block_cols(m),
                                 start=True, stop=True).then_inc(s_full, 1)

            def block_cols(m):
                r = (m % 4) * BLK
                return emb_t[m // 4][:, r:r + BLK, :].rearrange("p b d -> p (b d)")

            def spread(jb, u):
                m, pos = divmod(u, SLOTS)
                bank = v_ps[u % NV_BANKS]
                await_slot(jb, u)
                if pos == ECOL:
                    for g in range(GROUPS):
                        mm = nc.tensor.matmul(bank[:, g * FE:(g + 1) * FE], block_cols(m)[:, g * P:(g + 1) * P],
                                              pick_sb[:, E_AT:E_AT + FE], start=True, stop=True)
                else:
                    t = chunk(pos)
                    mm = nc.tensor.matmul(bank[0:CH, :], pick_sb[:, t * CH:(t + 1) * CH], block_cols(m),
                                          start=True, stop=True)
                mm.then_inc(v_full, 1)

            def main(jb, m, pos):
                t = chunk(pos)
                await_slot(jb, m * SLOTS + pos, NV_BANKS)
                if t == 0:
                    pe.wait_ge(x1_ready, jb * STEPS + (m + 1))
                mm = nc.tensor.matmul(x1_ps[:, :], w0s[:, t, :], prod[(m * NCH + t) % NPROD][:, :],
                                      start=(t == 0), stop=(t == NCH - 1))
                mm.then_inc(prod_free, 1)

            def x1_turn(ph, jb, m):
                pe.wait_ge(x1_ready, jb * STEPS + (m + 1))
                bank = s_bank(ph, ("x1t", m))
                for g in range(GROUPS):
                    mm = nc.tensor.transpose(bank[:, g * P:(g + 1) * P], x1[(m - 1) % 2][:, g * P:(g + 1) * P],
                                             idf[:, :])
                mm.then_inc(s_full, 1)

            def interact(ph, jb, m, g):
                if g == 0:
                    await_drained(ph, ("x1t", m))
                    await_slot(jb, (m - 1) * SLOTS + ECOL, NV_BANKS)
                bank = s_bank(ph, (f"g{g}", m))
                nc.tensor.matmul(bank[:, 0:GRP * FE], x1t[(m - 1) % 2][:, g, :],
                                 ediag[(m - 1) % 2][:, g, :, :].rearrange("p b f -> p (b f)"),
                                 start=True, stop=True).then_inc(s_full, 1)

            def layer1(ph, m):
                await_drained(ph, ("g3", m))
                bank = s_bank(ph, ("z2", m))
                for f in range(FIELDS):
                    mm = nc.tensor.matmul(bank[:, 0:ROWS], w1_sb[:, f, :], g_sb[:, f, :],
                                          start=(f == 0), stop=(f == FIELDS - 1))
                mm.then_inc(s_full, 1)

            def hidden1(ph, m, jb, half):
                if half == 0:
                    await_drained(ph, ("z2", m))
                bank = s_bank(ph, (("h1a", "h1b")[half], m))
                rows = (g_sb[:, FIELDS, :], z2[:, :], dense_sb[:, bass.ds(jb * ROWS, ROWS)])
                for i in range(2):
                    mt = half * 2 + i
                    for k in range(KT1):
                        mm = nc.tensor.matmul(bank[:, i * ROWS:(i + 1) * ROWS], wt1[:, k, mt * P:(mt + 1) * P],
                                              rows[k], start=(k == 0), stop=(k == KT1 - 1))
                mm.then_inc(s_full, 1)

            def hidden2(ph, m):
                await_drained(ph, ("h1b", m))
                bank = s_bank(ph, ("h2", m))
                for mt in range(MT2):
                    for k in range(MT1):
                        mm = nc.tensor.matmul(bank[:, mt * ROWS:(mt + 1) * ROWS], wt2[:, k, mt * P:(mt + 1) * P],
                                              h1[:, k, :], start=(k == 0), stop=(k == MT1 - 1))
                mm.then_inc(s_full, 1)

            def score(ph, m):
                await_drained(ph, ("h2", m))
                bank = s_bank(ph, ("y", m))
                for k in range(MT2):
                    mm = nc.tensor.matmul(bank[:, 0:ROWS], wt3[:, k, :], h2[:, k, :],
                                          start=(k == 0), stop=(k == MT2 - 1))
                mm.then_inc(s_full, 1)

            def opening(ph):
                pe.sem_inc(prod_free, NPROD)
                pe.wait_ge(loads, 16 * len(LOADS))
                turns_ready(0)
                turn(ph, 0, 0)
                turn(ph, 0, 1)
                await_drained(ph, ("turn1", 0))
                spread_a(ph, -1, 0)
                for u in range(LEAD):
                    spread(0, u)
                pe.wait_ge(w0_ready, 1)

            def step(ph, jb, m):
                is_last = ph.order is LAST
                before = not (ph.order is FIRST)
                ends = before and m % STEPS == 0
                j_end = jb if m == STEPS else jb - 1
                for pos in range(SLOTS):
                    if m < STEPS:
                        if pos != ECOL:
                            main(jb, m, pos)
                        if pos == SLOTS - LEAD and ("opa", m) in ph.order:
                            if ("turn1", m) in ph.order and m:
                                await_drained(ph, ("turn1", m))
                            spread_a(ph, m, (m + 1) % STEPS)
                        u = m * SLOTS + pos + LEAD
                        if u < V_USES:
                            spread(jb, u)
                        elif not is_last:
                            spread(jb + 1, u - V_USES)
                    if not before:
                        continue
                    if pos == 0:
                        x1_turn(ph, jb, m)
                    elif pos == 2:
                        interact(ph, jb, m, 0)
                        interact(ph, jb, m, 1)
                    elif pos == 3:
                        interact(ph, jb, m, 2)
                        interact(ph, jb, m, 3)
                    if ("turn0", m) in ph.order and m % 4 == 3 and pos in (3, 4):
                        if pos == 3:
                            turns_ready(jb * 2 + (m + 1) // 4)
                        turn(ph, m, pos - 3)
                    if ends and pos == 4:
                        layer1(ph, m)
                    elif ends and pos == 5:
                        hidden1(ph, m, j_end, 0)
                        hidden1(ph, m, j_end, 1)
                    elif ends and pos == 6:
                        hidden2(ph, m)
                    elif ends and pos == 7:
                        score(ph, m)
            phases(pe, opening, step)

        @block.scalar
        def _(act):
            def drain(ph, use):
                act.wait_ge(s_full, ph.count(use))
                return s_ps[ph.bank(use)]

            def parts_of(jt, t, n):
                if n == 0:
                    act.wait_ge(gathered[t], jt * (16 * FIELDS) + 16 * FIELDS)
                else:
                    act.wait_ge(rest_ready, jt * 2 + (t + 3))
                nc.scalar.copy(parts[:, :, n, :], (emb[t] if n == 0 else rest)[:, :, :].rearrange("p f d -> p d f")
                               ).then_inc((part0_ready, part1_ready)[n], 1)

            def turn(ph, m, t, half):
                bank = drain(ph, (f"turn{half}", m))
                nc.scalar.copy(emb_t[t][:, :, half * HALF:(half + 1) * HALF].rearrange("p b d -> p d b"),
                               bank[:, :].bitcast(BF16)[0:CH, :].rearrange("p (d b) -> p d b", d=HALF)
                               ).then_inc(s_drained, 1)

            def operand_a(ph, m_step, m):
                bank = drain(ph, ("opa", m_step))
                nc.scalar.copy(opa[m % 2][:, :], bank[0:CH, :]).then_inc(s_drained, 1)

            def opening(ph):
                act.sem_inc(s_drained, NS_BANKS)
                act.sem_inc(x1_ready, 1)
                act.wait_ge(loads, 16 * len(LOADS))
                parts_of(0, 0, 0)
                parts_of(0, 0, 1)
                turn(ph, 0, 0, 0)
                turn(ph, 0, 0, 1)
                operand_a(ph, -1, 0)

            def step(ph, jb, m):
                before = not (ph.order is FIRST)
                ends = before and m % STEPS == 0
                j_end = jb if m == STEPS else jb - 1
                turning = ("turn0", m) in ph.order and m % 4 == 3
                next_tile = (jb if m == 3 else jb + 1, 1 if m == 3 else 0)
                if before:
                    act.wait_ge(prod_free, jb * PROD + (m * NCH + NPROD))
                    nc.scalar.copy(x1[(m - 1) % 2][:, :], x1_ps[:, :]).then_inc(x1_ready, 1)
                    bank = drain(ph, ("x1t", m))
                    nc.scalar.copy(x1t[(m - 1) % 2][:, :, :].rearrange("p g h -> p (g h)"),
                                   bank[:, :]).then_inc(s_drained, 1)
                if turning:
                    parts_of(*next_tile, 0)
                    parts_of(*next_tile, 1)
                if before:
                    for g in range(GROUPS):
                        bank = drain(ph, (f"g{g}", m))
                        r = ((m - 1) % STEPS) * BLK + g * GRP
                        nc.scalar.copy(g_sb[:, :, r:r + GRP].rearrange("p f b -> p b f"),
                                       bank[:, 0:GRP * FE].rearrange("p (b f) -> p b f", b=GRP)
                                       ).then_inc(s_drained, 1)
                if turning:
                    turn(ph, m, next_tile[1], 0)
                    turn(ph, m, next_tile[1], 1)
                if ends:
                    bank = drain(ph, ("z2", m))
                    nc.scalar.copy(z2[:, :], bank[:, 0:ROWS]).then_inc(s_drained, 1)
                if ("opa", m) in ph.order:
                    operand_a(ph, m, (m + 1) % STEPS)
                if ends:
                    for use, dst, bias, n in (("h1a", h1, bt1, 0), ("h1b", h1, bt1, 2), ("h2", h2, bt2, 0)):
                        bank = drain(ph, (use, m))
                        for i in range(2):
                            a = nc.scalar.activation(dst[:, n + i, :], bank[:, i * ROWS:(i + 1) * ROWS], ACT.Relu,
                                                     bias=bias[:, n + i:n + i + 1])
                        a.then_inc(s_drained, 1)
                    bank = drain(ph, ("y", m))
                    nc.scalar.copy(y[:, bass.ds(j_end * ROWS, ROWS)], bank[0:1, 0:ROWS]).then_inc(s_drained, 1)

            phases(act, opening, step)

        @block.vector
        def _(dve):
            def parts_of(jt, t):
                dve.wait_ge(part0_ready, jt * 2 + (t + 1))
                nc.vector.tensor_tensor(rest[:, :, :], emb[t][:, :, :], parts[:, :, 0, :].rearrange("p d f -> p f d"),
                                        ALU.subtract).then_inc(rest_ready, 1)

            def part2_of(jt, t):
                dve.wait_ge(part1_ready, jt * 2 + (t + 1))
                nc.vector.tensor_tensor(parts[:, :, 2, :], rest[:, :, :].rearrange("p f d -> p d f"),
                                        parts[:, :, 1, :], ALU.subtract).then_inc(part2_ready, 1)

            def multiply(ph, jb, m, pos):
                q = m * NCH + chunk(pos)
                if pos == 0 and m == 1:
                    dve.wait_ge(s_drained, ph.count(ph.order[0]) - 1 + NS_BANKS)
                elif pos == 0:
                    dve.wait_ge(s_drained, NS_BANKS + ph.count(("opa", m - 1 if m else (-1 if ph.order is FIRST else 7))))
                dve.wait_ge(prod_free, jb * PROD + (q + 1))
                dve.wait_ge(v_full, jb * V_USES + (m * SLOTS + pos + 1))
                nc.vector.tensor_tensor(prod[q % NPROD][:, :], opa[m % 2][:, :], v_ps[pos % NV_BANKS][0:CH, :],
                                        ALU.mult).then_inc(v_drained, 1)

            def own_blocks(ph, jb, m):
                if ph.order is not FIRST:
                    dve.wait_ge(s_drained, NS_BANKS + ph.count(("x1t", m)))
                dve.wait_ge(v_full, jb * V_USES + (m * SLOTS + ECOL + 1))
                shape = [P, GROUPS, GRP, FIELDS]
                cols = v_ps[ECOL % NV_BANKS][:, 0:GROUPS * FE].rearrange("p (g f) -> p g f", g=GROUPS)[:, :, 0:FIELDS]
                nc.vector.tensor_tensor(ediag[m % 2][:, :, :, 0:FIELDS], cols.unsqueeze(2).to_broadcast(shape),
                                        own[:, :].unsqueeze(1).unsqueeze(3).to_broadcast(shape),
                                        ALU.mult).then_inc(v_drained, 1)

            def opening(ph):
                dve.sem_inc(v_drained, NV_BANKS)
                dve.sem_inc(rest_ready, 2)

                nc.vector.memset(wt1[:, KT1 - 1, :], 0.0).then_inc(pads_ready, 1)
                nc.vector.memset(dense_sb[:, :], 0.0).then_inc(pads_ready, 1)
                dve.wait_ge(loads, 16 * len(LOADS))
                nc.vector.tensor_tensor(w0s[:, :, :], w0a[:, :, :], w0b[:, :, :], ALU.add).then_inc(w0_ready, 1)
                for i in range(2):
                    nc.vector.tensor_copy(ediag[i][:, :, :, FIELDS],
                                          own[:, :].unsqueeze(1).to_broadcast([P, GROUPS, GRP]))
                parts_of(0, 0)
                part2_of(0, 0)

            def step(ph, jb, m):
                if m == STEPS:
                    return
                turning = ("turn0", m) in ph.order and m % 4 == 3
                next_tile = (jb if m == 3 else jb + 1, 1 if m == 3 else 0)
                for pos in range(SLOTS):
                    if pos == ECOL:
                        own_blocks(ph, jb, m)
                    else:
                        multiply(ph, jb, m, pos)
                    if turning and pos == 0:
                        parts_of(*next_tile)
                    elif turning and pos == 1:
                        part2_of(*next_tile)

            phases(dve, opening, step)


def _constants():
    one = 0x3F80
    part_field = np.arange(CH) % FIELDS
    wanted = [(np.arange(CH) % FIELDS + SHIFTS * t + np.arange(CH) // FIELDS) % FIELDS for t in range(NCH)]
    wanted += [np.arange(CH) % FIELDS, np.arange(FE)]
    pick = np.where(part_field[:, None] == np.concatenate(wanted)[None, :], one, 0).astype(np.uint16)
    own_rows = (np.arange(P)[:, None] // D == np.arange(GRP)[None, :]).astype(np.float32)
    return {"pick": pick, "ident_bf": np.where(np.eye(P) == 1, one, 0).astype(np.uint16),
            "ident_f": np.eye(P, dtype=np.float32), "own_rows": own_rows}


def _pair_weights(w0):
    w = w0.reshape(H, FIELDS, FIELDS)
    ij = np.zeros((CH, NCH, H), w0.dtype)
    ji = np.zeros((CH, NCH, H), w0.dtype)
    i = np.arange(FIELDS)
    for t in range(NCH):
        for k in range(SHIFTS):
            s = SHIFTS * t + k
            rows = slice(k * FIELDS, (k + 1) * FIELDS)
            j = (i + s) % FIELDS
            ij[rows, t] = w[:, i, j].T
            if 0 < s < FIELDS // 2:
                ji[rows, t] = w[:, j, i].T
    return ij, ji


def kernel(**inputs):
    import concourse.bacc as bacc
    from concourse.bass_utils import run_bass_kernel_spmd

    a = {k: np.ascontiguousarray(v) for k, v in inputs.items()}
    arrays = {"ids": a["ids"].reshape(TILES, P, FIELDS)}
    arrays |= {f"tbl_{f}": a[f"tbl_{f}"] for f in range(FIELDS)}
    arrays["dense_t"] = np.ascontiguousarray(a["dense_ctx"].T)
    arrays["w0_ij"], arrays["w0_ji"] = _pair_weights(a["L0_rec_W0"])
    arrays["w1_t"] = np.ascontiguousarray(a["L0_rec_W1"].reshape(H, H, FIELDS).transpose(1, 2, 0))
    arrays |= {"w_top1": a["W_top1"], "w_top2": a["W_top2"], "w_top3": np.pad(a["W_top3"], ((0, 0), (0, P - 1))),
               "b_top1": np.ascontiguousarray(a["b_top1"].reshape(MT1, P).T),
               "b_top2": np.ascontiguousarray(a["b_top2"].reshape(MT2, P).T)}
    arrays |= _constants()

    nc = bacc.Bacc("TRN2", target_bir_lowering=False, num_devices=1)
    ap = {k: nc.dram_tensor(k, v.shape, mybir.dt.from_np(v.dtype), kind="ExternalInput").ap()
          for k, v in arrays.items()}
    out = nc.dram_tensor("score", (1, B), F32, kind="ExternalOutput").ap()
    tables = [ap.pop(f"tbl_{f}") for f in range(FIELDS)]
    cin_tower(nc, tables=tables, out=out, **ap)
    r = run_bass_kernel_spmd(nc, [arrays], core_ids=[0])
    return r.results[0]["score"].reshape(B, 1)
```

```python
from contextlib import ExitStack

import concourse.bass as bass
import numpy as np
from concourse import mybir

F32 = mybir.dt.float32
F32R = mybir.dt.float32r
BF16 = mybir.dt.bfloat16
I32 = mybir.dt.int32
ALU = mybir.AluOpType
ACT = mybir.ActivationFunctionType

B, FIELDS, D, H = 1024, 39, 16, 128
HID1, HID2 = 512, 256
P = 128
BANK = 512
TILES = B // P
COLS = P * D
SHIFTS = 3
CH = SHIFTS * FIELDS
NCH = -(-(FIELDS // 2 + 1) // SHIFTS)
UNITS = 2 * NCH
HALF = COLS // 2
GRP = P // D
QUARTERS = COLS // BANK
GROUPS = BANK // P
FE = FIELDS + 1
A_AT, E_AT = 0, CH
DT = BANK * 2 // P
KT1, MT1 = 3, HID1 // P
MT2 = HID2 // P
NS, NB, NP, NX = 3, 4, 4, 2
HIGH_LEAD = 2
OWN_LAG = 2


def beside_units():
    work = [("x1t0", 0, 2 * BANK)]
    for q in range(QUARTERS):
        if q + 1 < QUARTERS:
            work += [("ecols", q + 1, P), (f"x1t{q + 1}", 0, 2 * BANK)]
        for g in range(GROUPS):
            if q == QUARTERS - 1 and g < 2:
                work.append((f"turn{g}", 0, DT * P))
            work.append((f"g{q * GROUPS + g}", 0, 4 * GRP * FE))
    work += [(f"a{q}", 0, BANK) for q in range(QUARTERS)]
    work += [("z2", f, 4 * P) for f in range(FIELDS)]
    work += [("h1", m, 4 * KT1 * P) for m in range(MT1)] + [("h2", m, 4 * MT1 * P) for m in range(MT2)]
    work += [("y", 0, 4 * MT2 * P)]
    total, at, units = sum(w for *_, w in work), 0, [[] for _ in range(UNITS)]
    for piece, n, w in work:
        units[(at + w // 2) * UNITS // total].append((piece, n))
        at += w
    return units


BESIDE = beside_units()
LAST_PIECE = {"z2": FIELDS - 1, "h1": MT1 - 1, "h2": MT2 - 1}
PREPARE = ("turn0", "turn1", "a0", "a1", "a2", "a3")


def unit_of(piece, n=0):
    return next(u for u in range(UNITS) if (piece, n) in BESIDE[u])


ECOLS0_AT = UNITS - 5
SPLIT_AT = unit_of("turn0") - 2


def scalar_uses(previous, following):
    pieces = dict.fromkeys(piece for unit in BESIDE for piece, _ in unit if piece != "ecols")
    return [x for x in pieces if (following if x in PREPARE else previous)]


FULL, FINAL = scalar_uses(True, True), scalar_uses(True, False)
assert len(PREPARE) % NS == 0 and len(FULL) % NS == 0 and len(FINAL) % NS == 0


class Step:

    def __init__(self, i, t, kind="full"):
        self.i, self.t = i, t
        self.layer0 = kind != "tail"
        self.previous = kind != "first"
        self.following = kind in ("first", "full")
        self.order = scalar_uses(self.previous, self.following)
        self.before = (len(PREPARE) if kind == "first" else
                       2 * len(PREPARE) + (TILES - 2) * len(FULL) + len(FINAL) if kind == "tail" else
                       i * (2 * len(FULL)) + (2 * len(PREPARE) + (t - 1) * len(FULL)))

    def tile(self, scale, plus):
        return self.i * (2 * scale) + (self.t * scale + plus)

    def count_before(self, use):
        order = FULL if self.layer0 else FINAL
        return self.before + (order.index(use) + 1 - len(order))

    def count(self, use):
        return self.before + (self.order.index(use) + 1)


def slot(s, u, tiles_on=0):
    return ((s.t + tiles_on) * UNITS + u) % NP


class Opening(Step):

    def __init__(self):
        super().__init__(0, -1, "first")
        self.before = 0


def steps(eng, opening, step):
    opening(Opening())
    step(Step(0, 0, "first"))
    with eng.Fori(0, TILES // 2 - 1) as j:
        step(Step(j, 1))
        step(Step(j + 1, 0))
    step(Step(TILES // 2 - 1, 1, "final"))
    step(Step(TILES // 2, 0, "tail"))


def cin_tower(nc, ids, tables, dense_t, w0_ij, w0_ji, w1_t, w_top1, w_top2, w_top3, b_top1, b_top2,
              pick, ident_bf, ident_f, own_rows, out):
    with ExitStack() as ctx:
        def sb(name, shape, dt=F32):
            return ctx.enter_context(nc.sbuf_tensor(name, shape, dt))

        def psum(name, shape):
            return ctx.enter_context(nc.psum_tensor(name, shape, F32))

        def sem(name):
            return ctx.enter_context(nc.semaphore(name))

        pick_sb = sb("pick_sb", [CH, CH + FE], BF16)
        idb = sb("idb", [P, P], BF16)
        idf = sb("idf", [P, P])
        own = sb("own", [P, GRP])
        w0h = sb("w0h", [CH, NCH, H], F32R)
        w0l = sb("w0l", [CH, NCH, H], F32R)
        w1_sb = sb("w1_sb", [H, FIELDS, H])
        wt1 = sb("wt1", [P, KT1, HID1])
        wt2 = sb("wt2", [P, MT1, HID2])
        wt3 = sb("wt3", [P, MT2, P])
        bt1 = sb("bt1", [P, MT1])
        bt2 = sb("bt2", [P, MT2])
        dense_sb = sb("dense_sb", [P, B])
        idx = [sb(f"idx{t}", [P, FIELDS], I32) for t in range(2)]
        emb = [sb(f"emb{t}", [P, FIELDS, D]) for t in range(2)]
        rest = sb("rest", [P, FIELDS, D])
        parts = sb("parts", [P, D, 3, FIELDS], BF16)
        emb_t = [sb(f"emb_t{t}", [CH, P, D], BF16) for t in range(2)]
        opa = [sb(f"opa{t}", [CH, COLS]) for t in range(2)]
        opb = [sb(f"opb{n}", [CH, HALF]) for n in range(NB)]
        prod = [sb(f"prod{n}", [CH, HALF]) for n in range(NP)]
        prod_h = [sb(f"prod_h{n}", [CH, HALF], F32R) for n in range(NP)]
        prod_l = [sb(f"prod_l{n}", [CH, HALF], F32R) for n in range(NP)]
        x1 = sb("x1", [H, COLS])
        x1t = [sb(f"x1t{n}", [P, GROUPS, H]) for n in range(2)]
        ediag = [sb(f"ediag{n}", [P, GROUPS, GRP, FE]) for n in range(2)]
        g_sb = sb("g_sb", [H, FE, P])
        z2 = sb("z2", [H, P])
        h1 = sb("h1", [P, MT1, P])
        h2 = sb("h2", [P, MT2, P])
        y = sb("y", [1, B])
        w0_raw = [prod[n][:, 0:NCH * H].rearrange("p (c h) -> p c h", c=NCH) for n in range(2)]
        w0s = x1[0:CH, 0:NCH * H].rearrange("p (c h) -> p c h", c=NCH)

        x1_ps = psum("x1_ps", [P, COLS])
        s_ps = [psum(f"s_ps{n}", [P, BANK]) for n in range(NS)]
        ecol_ps = psum("ecol_ps", [P, BANK])

        loads = sem("loads")
        pads_ready = sem("pads_ready")
        w0_sum = sem("w0_sum")
        w0_high = sem("w0_high")
        w0_ready = sem("w0_ready")
        idx_ready = [sem(f"idx_ready{t}") for t in range(2)]
        tile_begun = sem("tile_begun")
        gathered = [sem(f"gathered{t}") for t in range(2)]
        part0_ready = sem("part0_ready")
        rest_ready = sem("rest_ready")
        part1_ready = sem("part1_ready")
        part2_ready = sem("part2_ready")
        s_full = sem("s_full")
        s_drained = sem("s_drained")
        a_ready = sem("a_ready")
        b_ready = [sem(f"b_ready{n}") for n in range(NB)]
        multiplied = sem("multiplied")
        high_ready = sem("high_ready")
        low_ready = sem("low_ready")
        unit_done = sem("unit_done")
        x1_ready = sem("x1_ready")
        ecol_full = sem("ecol_full")
        ediag_ready = sem("ediag_ready")
        y_stored = sem("y_stored")

        LOADS = [(pick_sb[:, :], pick.bitcast(BF16)), (idb[:, :], ident_bf.bitcast(BF16)),
                 (w0_raw[0], w0_ij), (w0_raw[1], w0_ji),
                 (idf[:, :], ident_f), (own[:, :], own_rows), (w1_sb[:, :, :], w1_t),
                 (wt2[:, :, :], w_top2.rearrange("(k p) n -> p k n", p=P)),
                 (wt3[:, :, :], w_top3.rearrange("(k p) n -> p k n", p=P)),
                 (bt1[:, :], b_top1), (bt2[:, :], b_top2),
                 (wt1[:, 0:2, :], w_top1[0:2 * P].rearrange("(k p) n -> p k n", p=P)),
                 (wt1[0:D, 2, :], w_top1[2 * P:2 * P + D]), (dense_sb[0:D, :], dense_t)]
        PADDED = 2

        block = ctx.enter_context(nc.Block())

        @block.sync
        def _(sp):
            def opening(_):
                for n, (dst, src) in enumerate(LOADS):
                    if n == len(LOADS) - PADDED:
                        sp.wait_ge(pads_ready, 2)
                    sp.dma_start(dst, src).then_inc(loads, 16)

            def step(s):
                if not s.layer0:
                    return
                for u in range(UNITS):
                    c, half = divmod(u, 2)
                    slot = (s.t * UNITS + u) % NB
                    cols = slice(half * HALF, (half + 1) * HALF)
                    if u == 0:
                        sp.wait_ge(a_ready, s.tile(1, 1))
                    sp.wait_ge(multiplied, s.tile(UNITS, u + 1))
                    for k in range(SHIFTS):
                        shift = SHIFTS * c + k
                        sp.dma_start(opb[slot][k * FIELDS:(k + 1) * FIELDS, :],
                                     opa[s.t][shift:shift + FIELDS, cols]).then_inc(b_ready[slot], 16)

            steps(sp, opening, step)
            tail = Step(TILES // 2, 0, "tail")
            sp.wait_ge(s_drained, tail.count("y") + NS)
            sp.dma_start(out, y[:, :]).then_inc(y_stored, 16)
            sp.wait_ge(y_stored, 16)

        @block.gpsimd
        def _(pool):
            nc.gpsimd.dma_start(idx[0][:, :], ids[0]).then_inc(idx_ready[0], 16)
            with pool.Fori(0, TILES // 2) as j:
                for t in range(2):
                    pool.wait_ge(idx_ready[t], j * 16 + 16)
                    pool.wait_ge(rest_ready, j * 2 + (t + 1))
                    pool.sem_inc(tile_begun, 1)
                    for f in range(FIELDS):
                        nc.gpsimd.indirect_dma_start(emb[t][:, f, :], None, tables[f],
                                                     bass.IndirectOffsetOnAxis(idx[t][:, f:f + 1], 0)
                                                     ).then_inc(gathered[t], 16)
                        if f == FIELDS // 2:
                            pool.wait_ge(rest_ready, j * 2 + (t + 2))
                            pool.sem_inc(tile_begun, 1)
                            nc.gpsimd.dma_start(idx[1 - t][:, :], ids[bass.ds(j * 2 + (t + 1), 1)].rearrange(
                                "a p f -> (a p) f")).then_inc(idx_ready[1 - t], 16)
            pool.wait_ge(idx_ready[0], (TILES // 2 + 1) * 16)

        @block.tensor
        def _(pe):
            def ring(s, use):
                pe.wait_ge(s_drained, s.count(use))
                return s_ps[s.order.index(use) % NS]

            def await_drained(s, use):
                pe.wait_ge(s_drained, s.count(use) + NS)

            def turn(s, half):
                bank = ring(s, f"turn{half}")[:, :].bitcast(BF16)
                if half == 0:
                    for part in (part0_ready, part1_ready, part2_ready):
                        pe.wait_ge(part, s.tile(1, 2))
                for d in range(DT):
                    mm = nc.tensor.transpose(bank[0:CH, d * P:(d + 1) * P],
                                             parts[:, half * DT + d, :, :].rearrange("p a f -> p (a f)"), idb[:, :])
                mm.then_inc(s_full, 1)

            def quarter(t, q):
                return emb_t[t][:, :, :].rearrange("p b d -> p (b d)")[:, q * BANK:(q + 1) * BANK]

            def operand_a(s, q):
                if q == 0:
                    await_drained(s, "turn1")
                nc.tensor.matmul(ring(s, f"a{q}")[0:CH, :], pick_sb[:, A_AT:A_AT + CH], quarter(1 - s.t if s.t >= 0 else 0, q),
                                 start=True, stop=True).then_inc(s_full, 1)

            def unit(s, u):
                c, half = divmod(u, 2)
                pe.wait_ge(low_ready, s.tile(UNITS, u + 1))
                if c == 0:
                    pe.wait_ge(x1_ready, s.tile(NX, half + 1))
                n = slot(s, u)
                passes = ((w0h, prod_h[n]), (w0h, prod_l[n]), (w0l, prod_h[n]))
                for k, (w, x) in enumerate(passes):
                    for q in range(2):
                        mm = nc.tensor.matmul(x1_ps[:, half * HALF + q * BANK:half * HALF + (q + 1) * BANK],
                                              w[:, c, :], x[:, q * BANK:(q + 1) * BANK],
                                              start=(c == 0 and k == 0),
                                              stop=(c == NCH - 1 and k == len(passes) - 1))
                mm.then_inc(unit_done, 1)

            def ecols(s, q):
                t = s.t if q == 0 else 1 - s.t
                pe.wait_ge(ediag_ready, s.tile(QUARTERS, (q or QUARTERS) - QUARTERS + 1))
                for g in range(GROUPS):
                    mm = nc.tensor.matmul(ecol_ps[:, g * FE:(g + 1) * FE], quarter(t, q)[:, g * P:(g + 1) * P],
                                          pick_sb[:, E_AT:E_AT + FE], start=True, stop=True)
                mm.then_inc(ecol_full, 1)

            def x1_turn(s, q):
                pe.wait_ge(x1_ready, s.tile(NX, q // 2 + 1))
                bank = ring(s, f"x1t{q}")
                for g in range(GROUPS):
                    at = (q * GROUPS + g) * P
                    mm = nc.tensor.transpose(bank[:, g * P:(g + 1) * P], x1[:, at:at + P], idf[:, :])
                mm.then_inc(s_full, 1)

            def interact(s, n):
                q, g = divmod(n, GROUPS)
                if g == 0:
                    await_drained(s, f"x1t{q}")
                    pe.wait_ge(ediag_ready, s.tile(QUARTERS, q - QUARTERS + 2))
                nc.tensor.matmul(ring(s, f"g{n}")[:, 0:GRP * FE], x1t[q % 2][:, g, :],
                                 ediag[q % 2][:, g, :, :].rearrange("p b f -> p (b f)"),
                                 start=True, stop=True).then_inc(s_full, 1)

            def layer1(s, f):
                if f == 0:
                    await_drained(s, f"g{QUARTERS * GROUPS - 1}")
                    ring(s, "z2")
                mm = nc.tensor.matmul(s_ps[s.order.index("z2") % NS][:, 0:P], w1_sb[:, f, :], g_sb[:, f, :],
                                      start=(f == 0), stop=(f == FIELDS - 1))
                if f == FIELDS - 1:
                    mm.then_inc(s_full, 1)

            def dense_layer(s, use, needs, w, rows, m, outs):
                if m == 0:
                    await_drained(s, needs)
                    ring(s, use)
                for k, x in enumerate(rows):
                    mm = nc.tensor.matmul(s_ps[s.order.index(use) % NS][:, m * P:(m + 1) * P],
                                          w[:, k, m * P:(m + 1) * P], x,
                                          start=(k == 0), stop=(k == len(rows) - 1))
                if m == outs - 1:
                    mm.then_inc(s_full, 1)

            def beside(s, u):
                for piece, n in BESIDE[u]:
                    if not (s.following if piece in PREPARE else s.previous):
                        continue
                    if piece == "ecols":
                        ecols(s, n)
                    elif piece == "z2":
                        layer1(s, n)
                    elif piece == "h1":
                        dense_layer(s, "h1", "z2", wt1, (g_sb[:, FIELDS, :], z2[:, :],
                                                         dense_sb[:, bass.ds(s.tile(P, -P), P)]), n, MT1)
                    elif piece == "h2":
                        dense_layer(s, "h2", "h1", wt2, [h1[:, k, :] for k in range(MT1)], n, MT2)
                    elif piece == "y":
                        dense_layer(s, "y", "h2", wt3, [h2[:, k, :] for k in range(MT2)], n, 1)
                    elif piece.startswith("x1t"):
                        x1_turn(s, int(piece[3:]))
                    elif piece.startswith("turn"):
                        turn(s, int(piece[4:]))
                    elif piece.startswith("a"):
                        operand_a(s, int(piece[1:]))
                    elif piece.startswith("g"):
                        interact(s, int(piece[1:]))

            def opening(s):
                pe.sem_inc(unit_done, NP)
                pe.wait_ge(loads, 16 * len(LOADS))
                turn(s, 0)
                turn(s, 1)
                for q in range(QUARTERS):
                    operand_a(s, q)
                pe.wait_ge(w0_ready, 1)

            def step(s):
                for u in range(UNITS):
                    if s.layer0:
                        unit(s, u)
                    beside(s, u)
                    if s.layer0 and u == ECOLS0_AT:
                        ecols(s, 0)

            steps(pe, opening, step)

        @block.scalar
        def _(act):
            def full(s, use):
                act.wait_ge(s_full, s.count(use))
                return s_ps[s.order.index(use) % NS]

            def split(s, n):
                t = 1 - s.t if s.t >= 0 else 0
                if n == 0:
                    whole = s.i + s.t if s.t >= 0 else 0
                    act.wait_ge(gathered[t], whole * (16 * FIELDS) + 16 * FIELDS)
                else:
                    act.wait_ge(rest_ready, s.tile(1, 2 + 2))
                nc.scalar.copy(parts[:, :, n, :], (emb[t] if n == 0 else rest)[:, :, :].rearrange("p f d -> p d f")
                               ).then_inc((part0_ready, part1_ready)[n], 1)

            def turned(s, half):
                t = 1 - s.t if s.t >= 0 else 0
                bank = full(s, f"turn{half}")
                nc.scalar.copy(emb_t[t][:, :, half * DT:(half + 1) * DT].rearrange("p b d -> p d b"),
                               bank[:, :].bitcast(BF16)[0:CH, :].rearrange("p (d b) -> p d b", d=DT)
                               ).then_inc(s_drained, 1)

            def operand_a(s, q):
                t = 1 - s.t if s.t >= 0 else 0
                nc.scalar.copy(opa[t][:, q * BANK:(q + 1) * BANK], full(s, f"a{q}")[0:CH, :]).then_inc(s_drained, 1)
                if q == QUARTERS - 1:
                    act.drain().then_inc(a_ready, 1)

            def high(s, u, tiles_on=0):
                act.wait_ge(multiplied, s.tile(UNITS, tiles_on * UNITS + u + 1 + NB))
                act.wait_ge(unit_done, s.tile(UNITS, tiles_on * UNITS + u + 1))
                n = slot(s, u, tiles_on)
                nc.scalar.copy(prod_h[n][:, :], prod[n][:, :]).then_inc(high_ready, 1)

            def x1_out(s, half):
                act.wait_ge(unit_done, s.tile(UNITS, UNITS - 1 + half + NP))
                cols = slice(half * HALF, (half + 1) * HALF)
                nc.scalar.copy(x1[:, cols], x1_ps[:, cols]).then_inc(x1_ready, 1)

            def g_out(s, n):
                nc.scalar.copy(g_sb[:, :, n * GRP:(n + 1) * GRP].rearrange("p f b -> p b f"),
                               full(s, f"g{n}")[:, 0:GRP * FE].rearrange("p (b f) -> p b f", b=GRP)
                               ).then_inc(s_drained, 1)

            def relu(s, use, dst, bias, outs):
                bank = full(s, use)
                for m in range(outs):
                    a = nc.scalar.activation(dst[:, m, :], bank[:, m * P:(m + 1) * P], ACT.Relu, bias=bias[:, m:m + 1])
                a.then_inc(s_drained, 1)

            def beside(s, u):
                for use in s.order:
                    if unit_of(use, LAST_PIECE.get(use, 0)) != u:
                        continue
                    if use.startswith("x1t"):
                        q = int(use[3:])
                        nc.scalar.copy(x1t[q % 2][:, :, :].rearrange("p g h -> p (g h)"), full(s, use)[:, :]
                                       ).then_inc(s_drained, 1)
                    elif use.startswith("g"):
                        g_out(s, int(use[1:]))
                    elif use.startswith("turn"):
                        turned(s, int(use[4:]))
                    elif use.startswith("a"):
                        operand_a(s, int(use[1:]))
                    elif use == "z2":
                        nc.scalar.copy(z2[:, :], full(s, use)[:, 0:P]).then_inc(s_drained, 1)
                    elif use == "h1":
                        relu(s, use, h1, bt1, MT1)
                    elif use == "h2":
                        relu(s, use, h2, bt2, MT2)
                    elif use == "y":
                        nc.scalar.copy(y[:, bass.ds(s.tile(P, -P), P)], full(s, use)[0:1, 0:P]).then_inc(s_drained, 1)

            def opening(s):
                act.sem_inc(s_drained, NS)
                act.sem_inc(x1_ready, NX)
                split(s, 0)
                split(s, 1)
                act.wait_ge(w0_sum, 1)
                nc.scalar.copy(w0h[:, :, :], w0s).then_inc(w0_high, 1)
                for half in range(2):
                    turned(s, half)
                for q in range(QUARTERS):
                    operand_a(s, q)
                for u in range(HIGH_LEAD):
                    high(s, u, 1)

            def step(s):
                for u in range(UNITS):
                    if s.layer0 and u + HIGH_LEAD < UNITS:
                        high(s, u + HIGH_LEAD)
                    elif s.layer0 and s.following:
                        high(s, u + HIGH_LEAD - UNITS, 1)
                    if s.following and u == SPLIT_AT:
                        split(s, 0)
                    if s.following and u == SPLIT_AT + 1:
                        split(s, 1)
                    beside(s, u)
                    if s.layer0 and u >= UNITS - 2:
                        x1_out(s, u - (UNITS - 2))

            steps(act, opening, step)

        @block.vector
        def _(dve):
            def split(s, n):
                if n == 0:
                    t = 1 - s.t if s.t >= 0 else 0
                    dve.wait_ge(part0_ready, s.tile(1, 2))
                    nc.vector.tensor_tensor(rest[:, :, :], emb[t][:, :, :],
                                            parts[:, :, 0, :].rearrange("p d f -> p f d"),
                                            ALU.subtract).then_inc(rest_ready, 1)
                else:
                    dve.wait_ge(part1_ready, s.tile(1, 2))
                    nc.vector.tensor_tensor(parts[:, :, 2, :], rest[:, :, :].rearrange("p f d -> p d f"),
                                            parts[:, :, 1, :], ALU.subtract).then_inc(part2_ready, 1)

            def multiply(s, u):
                half, n = u % 2, s.t * UNITS + u
                if s.previous or u >= NP:
                    dve.wait_ge(low_ready, s.tile(UNITS, u + 1 - NP))
                dve.wait_ge(b_ready[n % NB], s.i * (2 * UNITS // NB * 16 * SHIFTS) + (n // NB + 1) * 16 * SHIFTS)
                nc.vector.tensor_tensor(prod[n % NP][:, :], opa[s.t][:, half * HALF:(half + 1) * HALF],
                                        opb[n % NB][:, :], ALU.mult).then_inc(multiplied, 1)

            def low(s, u, tiles_on=0):
                at = tiles_on * UNITS + u
                dve.wait_ge(unit_done, s.tile(UNITS, at + 1))
                dve.wait_ge(high_ready, s.tile(UNITS, at + 1))
                n = slot(s, u, tiles_on)
                nc.vector.tensor_tensor(prod_l[n][:, :], prod[n][:, :], prod_h[n][:, :].bitcast(F32),
                                        ALU.subtract).then_inc(low_ready, 1)

            def own_blocks(s, q):
                dve.wait_ge(s_drained, (s.count(f"x1t{q}") if q >= 2 else
                                        s.count_before(f"g{QUARTERS * GROUPS - 1}")) + NS)
                dve.wait_ge(ecol_full, s.tile(QUARTERS, q - QUARTERS + 1))
                shape = [P, GROUPS, GRP, FIELDS]
                cols = ecol_ps[:, 0:GROUPS * FE].rearrange("p (g f) -> p g f", g=GROUPS)[:, :, 0:FIELDS]
                nc.vector.tensor_tensor(ediag[q % 2][:, :, :, 0:FIELDS], cols.unsqueeze(2).to_broadcast(shape),
                                        own[:, :].unsqueeze(1).unsqueeze(3).to_broadcast(shape),
                                        ALU.mult).then_inc(ediag_ready, 1)

            def opening(s):
                dve.sem_inc(multiplied, NB)
                dve.sem_inc(rest_ready, 2)
                dve.sem_inc(ediag_ready, 1)
                nc.vector.memset(wt1[:, KT1 - 1, :], 0.0).then_inc(pads_ready, 1)
                nc.vector.memset(dense_sb[:, :], 0.0).then_inc(pads_ready, 1)
                dve.wait_ge(loads, 16 * len(LOADS))
                nc.vector.tensor_tensor(w0s, w0_raw[0], w0_raw[1], ALU.add).then_inc(w0_sum, 1)
                for n in range(2):
                    nc.vector.tensor_copy(ediag[n][:, :, :, FIELDS],
                                          own[:, :].unsqueeze(1).to_broadcast([P, GROUPS, GRP]))
                split(s, 0)
                split(s, 1)
                dve.wait_ge(w0_high, 1)
                nc.vector.tensor_tensor(w0l[:, :, :], w0s, w0h[:, :, :].bitcast(F32),
                                        ALU.subtract).then_inc(w0_ready, 1)

            def step(s):
                for u in range(UNITS):
                    if s.layer0:
                        multiply(s, u)
                    if u:
                        if s.layer0:
                            low(s, u - 1)
                    elif s.previous:
                        low(s, UNITS - 1, -1)
                    for q in range(QUARTERS):
                        if s.previous and u == (unit_of("ecols", q) + OWN_LAG if q else 0):
                            own_blocks(s, q)
                    if s.following and u == SPLIT_AT + HIGH_LEAD:
                        split(s, 0)
                    if s.following and u == SPLIT_AT + HIGH_LEAD + 1:
                        split(s, 1)

            steps(dve, opening, step)


def _constants():
    one = 0x3F80
    part_field = np.arange(CH) % FIELDS
    wanted = [np.arange(CH) % FIELDS, np.arange(FE)]
    pick = np.where(part_field[:, None] == np.concatenate(wanted)[None, :], one, 0).astype(np.uint16)
    own_rows = (np.arange(P)[:, None] // D == np.arange(GRP)[None, :]).astype(np.float32)
    return {"pick": pick, "ident_bf": np.where(np.eye(P) == 1, one, 0).astype(np.uint16),
            "ident_f": np.eye(P, dtype=np.float32), "own_rows": own_rows}


def _pair_weights(w0):
    w = w0.reshape(H, FIELDS, FIELDS)
    ij = np.zeros((CH, NCH, H), w0.dtype)
    ji = np.zeros((CH, NCH, H), w0.dtype)
    i = np.arange(FIELDS)
    for t in range(NCH):
        for k in range(SHIFTS):
            s = SHIFTS * t + k
            rows = slice(k * FIELDS, (k + 1) * FIELDS)
            j = (i + s) % FIELDS
            ij[rows, t] = w[:, i, j].T
            if 0 < s < FIELDS // 2:
                ji[rows, t] = w[:, j, i].T
    return ij, ji


def kernel(**inputs):
    import concourse.bacc as bacc
    from concourse.bass_utils import run_bass_kernel_spmd

    a = {k: np.ascontiguousarray(v) for k, v in inputs.items()}
    arrays = {"ids": np.pad(a["ids"], ((0, P), (0, 0))).reshape(TILES + 1, P, FIELDS)}
    arrays |= {f"tbl_{f}": a[f"tbl_{f}"] for f in range(FIELDS)}
    arrays["dense_t"] = np.ascontiguousarray(a["dense_ctx"].T)
    arrays["w0_ij"], arrays["w0_ji"] = _pair_weights(a["L0_rec_W0"])
    arrays["w1_t"] = np.ascontiguousarray(a["L0_rec_W1"].reshape(H, H, FIELDS).transpose(1, 2, 0))
    arrays |= {"w_top1": a["W_top1"], "w_top2": a["W_top2"], "w_top3": np.pad(a["W_top3"], ((0, 0), (0, P - 1))),
               "b_top1": np.ascontiguousarray(a["b_top1"].reshape(MT1, P).T),
               "b_top2": np.ascontiguousarray(a["b_top2"].reshape(MT2, P).T)}
    arrays |= _constants()

    nc = bacc.Bacc("TRN2", target_bir_lowering=False, num_devices=1)
    ap = {k: nc.dram_tensor(k, v.shape, mybir.dt.from_np(v.dtype), kind="ExternalInput").ap()
          for k, v in arrays.items()}
    out = nc.dram_tensor("score", (1, B), F32, kind="ExternalOutput").ap()
    tables = [ap.pop(f"tbl_{f}") for f in range(FIELDS)]
    cin_tower(nc, tables=tables, out=out, **ap)
    r = run_bass_kernel_spmd(nc, [arrays], core_ids=[0])
    return r.results[0]["score"].reshape(B, 1)
```

```python
from contextlib import ExitStack

import concourse.bass as bass
import numpy as np
from concourse import mybir

F32 = mybir.dt.float32
F32R = mybir.dt.float32r
BF16 = mybir.dt.bfloat16
I32 = mybir.dt.int32
ALU = mybir.AluOpType
ACT = mybir.ActivationFunctionType

B, FIELDS, D, H = 1024, 39, 16, 128
HID1, HID2 = 512, 256
P = 128
BANK = 512
TILES = B // P
COLS = P * D
SHIFTS = 3
CH = SHIFTS * FIELDS
NCH = -(-(FIELDS // 2 + 1) // SHIFTS)
UNITS = 2 * NCH
HALF = COLS // 2
GRP = P // D
QUARTERS = COLS // BANK
GROUPS = BANK // P
FE = FIELDS + 1
A_AT, E_AT = 0, CH
DT = BANK * 2 // P
KT1, MT1 = 3, HID1 // P
MT2 = HID2 // P
NS, NB, NP, NX = 3, 4, 4, 2
HIGH_LEAD = 2
OWN_LAG = 3
TURN_BEFORE = ("h1b", 0)
A_BEFORE = ("h2", 0)
A2_BEFORE = ("x1t1", 0)
SPLIT_LEAD = 2
FIRST_LEAD = 1
AFTER_A_UNIT = {"z2": "g15", "g8": "x1t2", "h1a": "z2", "h2": "h1b", "y": "h2"}
PREPARE = ("turn0", "turn1", "a0", "a1", "a2", "a3")
LAST_PIECE = {"h1a": MT1 // 2 - 1, "h1b": MT1 // 2 - 1, "h2": MT2 - 1}


def beside_units():
    def turn(q):
        return [(f"x1t{q}", 0, 2 * BANK)]

    def interact(q):
        return [(f"g{q * GROUPS + g}", 0, 4 * GRP * FE) for g in range(GROUPS)]

    def ecols(q):
        return [("ecols", q, P)]

    def dense(piece, outs, depth):
        return [(piece, m, 4 * depth * P) for m in range(outs)]

    work = ecols(3) + turn(2) + turn(3) + interact(2) + interact(3)
    work += [("z2", f, 4 * P) for f in range(FIELDS)]
    work += dense("h1a", MT1 // 2, KT1) + ecols(0) + dense("h1b", MT1 // 2, KT1) + turn(0)
    work += dense("h2", MT2, MT1) + ecols(1) + turn(1) + dense("y", 1, MT2)
    work += interact(0) + ecols(2) + interact(1)
    for before, pieces, w in ((TURN_BEFORE, PREPARE[:2], DT * P), (A_BEFORE, PREPARE[2:4], BANK),
                              (A2_BEFORE, PREPARE[4:], BANK)):
        at = next(n for n, (*piece, _) in enumerate(work) if tuple(piece) == before)
        work[at:at] = [(piece, 0, w) for piece in pieces]
    total, at, u, least, units = sum(w for *_, w in work), 0, 0, {}, [[] for _ in range(UNITS)]
    for piece, n, w in work:
        u = max(u, (at + w // 2) * UNITS // total, least.get(AFTER_A_UNIT.get(piece), -1) + 1)
        units[u].append((piece, n))
        least[piece] = u
        at += w
    return units


BESIDE_FIRST = {8: [("ecols", 0), ("x1t0", 0)],
                10: [(piece, 0) for piece in PREPARE],
                11: [("ecols", 1), ("x1t1", 0)] + [(f"g{n}", 0) for n in range(GROUPS)],
                12: [("ecols", 2)],
                13: [(f"g{n}", 0) for n in range(GROUPS, 2 * GROUPS)]}
BESIDE = beside_units()
OF_THIS_TILE = [("ecols", q) for q in range(3)] + [(f"x1t{q}", 0) for q in range(2)] + [
    (f"g{n}", 0) for n in range(2 * GROUPS)]


def unit_of(piece, n=0):
    return next(u for u in range(UNITS) if (piece, n) in BESIDE[u])


class Step:

    def __init__(self, i, t, kind="full"):
        self.i, self.t = i, t
        self.layer0 = kind != "tail"
        self.previous = kind != "first"
        self.following = kind in ("first", "full")
        self.order = self.scalar_uses()
        self.before = OPENING_USES if kind == "first" else (
            OPENING_USES + FIRST_USES + (t - 1) * FULL_USES + i * (2 * FULL_USES) if kind != "tail" else
            OPENING_USES + FIRST_USES + (TILES - 2) * FULL_USES + FINAL_USES)
        self.first_slot = OPENING_USES if kind == "first" else OPENING_USES + FIRST_USES

    def scalar_uses(self):
        return list(dict.fromkeys(piece for u in range(UNITS) for piece, _ in self.beside(u)
                                  if piece not in ("ecols", "z2")))

    @property
    def next_parity(self):
        return (self.t + 1) % 2

    def tile(self, scale, plus):
        return self.i * (2 * scale) + (self.t * scale + plus)

    def beside(self, u):
        return [(piece, n) for piece, n in (BESIDE[u] if self.previous else BESIDE_FIRST.get(u, []))
                if (self.following if piece in PREPARE else
                    self.layer0 if (piece, n) in OF_THIS_TILE else self.previous)]

    def own_blocks_at(self, q):
        return unit_of("ecols", q) + OWN_LAG + (UNITS if q == 3 else 0)

    def split_at(self):
        lead = SPLIT_LEAD if self.previous else FIRST_LEAD
        return next(u for u in range(UNITS) if ("turn0", 0) in self.beside(u)) - lead

    def count_before(self, use):
        return self.before + (FULL.index(use) + 1 - FULL_USES)

    def count(self, use):
        return self.before + (self.order.index(use) + 1)

    def ring_slot(self, use):
        return (self.first_slot + self.order.index(use)) % NS


def slot(s, u, tiles_on=0):
    return ((s.t + tiles_on) * UNITS + u) % NP


class Opening(Step):

    def __init__(self):
        super().__init__(0, -1, "first")
        self.order, self.before, self.first_slot = PREPARE, 0, 0


OPENING_USES = len(PREPARE)
FIRST_USES = FULL_USES = FINAL_USES = 0
FULL = Step(0, 1).order
FIRST_USES, FULL_USES, FINAL_USES = (len(Step(0, 0, "first").order), len(FULL), len(Step(0, 1, "final").order))
assert FULL_USES % NS == 0 and FINAL_USES % NS == 0
for use in ("g3", "g7"):
    for step in (Step(0, 0, "first"), Step(0, 1, "final")):
        assert step.order[::-1].index(use) >= FULL[::-1].index(use)


def steps(eng, opening, step):
    opening(Opening())
    step(Step(0, 0, "first"))
    with eng.Fori(0, TILES // 2 - 1) as j:
        step(Step(j, 1))
        step(Step(j + 1, 0))
    step(Step(TILES // 2 - 1, 1, "final"))
    step(Step(TILES // 2, 0, "tail"))


def cin_tower(nc, ids, tables, dense_t, w0_ij, w0_ji, w1_t, w_top1, w_top2, w_top3, b_top1, b_top2,
              pick, ident_bf, ident_f, own_rows, out):
    with ExitStack() as ctx:
        def sb(name, shape, dt=F32):
            return ctx.enter_context(nc.sbuf_tensor(name, shape, dt))

        def psum(name, shape):
            return ctx.enter_context(nc.psum_tensor(name, shape, F32))

        def sem(name):
            return ctx.enter_context(nc.semaphore(name))

        pick_sb = sb("pick_sb", [CH, CH + FE], BF16)
        idb = sb("idb", [P, P], BF16)
        idf = sb("idf", [P, P])
        own = sb("own", [P, GRP])
        w0h = sb("w0h", [CH, NCH, H], F32R)
        w0l = sb("w0l", [CH, NCH, H], F32R)
        w1_sb = sb("w1_sb", [H, FIELDS, H])
        wt1 = sb("wt1", [P, KT1, HID1])
        wt2 = sb("wt2", [P, MT1, HID2])
        wt3 = sb("wt3", [P, MT2, P])
        bt1 = sb("bt1", [P, MT1])
        bt2 = sb("bt2", [P, MT2])
        dense_sb = sb("dense_sb", [P, B])
        idx = [sb(f"idx{t}", [P, FIELDS], I32) for t in range(2)]
        emb = [sb(f"emb{t}", [P, FIELDS, D]) for t in range(2)]
        rest = sb("rest", [P, FIELDS, D])
        parts = sb("parts", [P, D, 3, FIELDS], BF16)
        emb_t = [sb(f"emb_t{t}", [CH, P, D], BF16) for t in range(2)]
        opa = [sb(f"opa{t}", [CH, COLS]) for t in range(2)]
        opb = [sb(f"opb{n}", [CH, HALF]) for n in range(NB)]
        prod = [sb(f"prod{n}", [CH, HALF]) for n in range(NP)]
        prod_h = [sb(f"prod_h{n}", [CH, HALF], F32R) for n in range(NP)]
        prod_l = [sb(f"prod_l{n}", [CH, HALF], F32R) for n in range(NP)]
        x1 = sb("x1", [H, COLS])
        x1t = [sb(f"x1t{n}", [P, GROUPS, H]) for n in range(2)]
        ediag = [sb(f"ediag{n}", [P, GROUPS, GRP, FE]) for n in range(2)]
        g_sb = sb("g_sb", [H, FE, P])
        z2 = sb("z2", [H, P])
        h1 = sb("h1", [P, MT1, P])
        h2 = sb("h2", [P, MT2, P])
        y = sb("y", [1, B])
        w0_raw = [prod[n][:, 0:NCH * H].rearrange("p (c h) -> p c h", c=NCH) for n in range(2)]
        w0s = x1[0:CH, 0:NCH * H].rearrange("p (c h) -> p c h", c=NCH)

        x1_ps = psum("x1_ps", [P, COLS])
        s_ps = [psum(f"s_ps{n}", [P, BANK]) for n in range(NS)]
        misc_ps = psum("misc_ps", [P, BANK])

        loads = sem("loads")
        pads_ready = sem("pads_ready")
        w0_sum = sem("w0_sum")
        w0_high = sem("w0_high")
        w0_ready = sem("w0_ready")
        idx_ready = [sem(f"idx_ready{t}") for t in range(2)]
        tile_begun = sem("tile_begun")
        gathered = [sem(f"gathered{t}") for t in range(2)]
        part0_ready = sem("part0_ready")
        rest_ready = sem("rest_ready")
        part1_ready = sem("part1_ready")
        part2_ready = sem("part2_ready")
        s_full = sem("s_full")
        s_drained = sem("s_drained")
        a_ready = [sem(f"a_ready{n}") for n in range(2)]
        b_ready = [sem(f"b_ready{n}") for n in range(NB)]
        multiplied = sem("multiplied")
        high_ready = sem("high_ready")
        low_ready = sem("low_ready")
        unit_done = sem("unit_done")
        x1_ready = sem("x1_ready")
        ecol_full = sem("ecol_full")
        ediag_ready = sem("ediag_ready")
        z2_full = sem("z2_full")
        z2_ready = sem("z2_ready")
        y_stored = sem("y_stored")

        LOADS = [(pick_sb[:, :], pick.bitcast(BF16)), (idb[:, :], ident_bf.bitcast(BF16)),
                 (w0_raw[0], w0_ij), (w0_raw[1], w0_ji),
                 (idf[:, :], ident_f), (own[:, :], own_rows), (w1_sb[:, :, :], w1_t),
                 (wt2[:, :, :], w_top2.rearrange("(k p) n -> p k n", p=P)),
                 (wt3[:, :, :], w_top3.rearrange("(k p) n -> p k n", p=P)),
                 (bt1[:, :], b_top1), (bt2[:, :], b_top2),
                 (wt1[:, 0:2, :], w_top1[0:2 * P].rearrange("(k p) n -> p k n", p=P)),
                 (wt1[0:D, 2, :], w_top1[2 * P:2 * P + D]), (dense_sb[0:D, :], dense_t)]
        PADDED = 2

        block = ctx.enter_context(nc.Block())

        @block.sync
        def _(sp):
            def opening(_):
                for n, (dst, src) in enumerate(LOADS):
                    if n == len(LOADS) - PADDED:
                        sp.wait_ge(pads_ready, 2)
                    sp.dma_start(dst, src).then_inc(loads, 16)

            def step(s):
                if not s.layer0:
                    return
                for u in range(UNITS):
                    half, c = divmod(u, NCH)
                    slot = (s.t * UNITS + u) % NB
                    cols = slice(half * HALF, (half + 1) * HALF)
                    if u == 0:
                        sp.wait_ge(a_ready[0], s.tile(1, 1))
                    sp.wait_ge(multiplied, s.tile(UNITS, u + 1))
                    for k in range(SHIFTS):
                        shift = SHIFTS * c + k
                        sp.dma_start(opb[slot][k * FIELDS:(k + 1) * FIELDS, :],
                                     opa[s.t][shift:shift + FIELDS, cols]).then_inc(b_ready[slot], 16)

            steps(sp, opening, step)
            tail = Step(TILES // 2, 0, "tail")
            sp.wait_ge(s_drained, tail.count("y") + NS)
            sp.dma_start(out, y[:, :]).then_inc(y_stored, 16)
            sp.wait_ge(y_stored, 16)

        @block.gpsimd
        def _(pool):
            nc.gpsimd.dma_start(idx[0][:, :], ids[0]).then_inc(idx_ready[0], 16)
            with pool.Fori(0, TILES // 2) as j:
                for t in range(2):
                    pool.wait_ge(idx_ready[t], j * 16 + 16)
                    pool.wait_ge(rest_ready, j * 2 + (t + 1))
                    pool.sem_inc(tile_begun, 1)
                    for f in range(FIELDS):
                        nc.gpsimd.indirect_dma_start(emb[t][:, f, :], None, tables[f],
                                                     bass.IndirectOffsetOnAxis(idx[t][:, f:f + 1], 0)
                                                     ).then_inc(gathered[t], 16)
                        if f == FIELDS // 2:
                            pool.wait_ge(rest_ready, j * 2 + (t + 2))
                            pool.sem_inc(tile_begun, 1)
                            nc.gpsimd.dma_start(idx[1 - t][:, :], ids[bass.ds(j * 2 + (t + 1), 1)].rearrange(
                                "a p f -> (a p) f")).then_inc(idx_ready[1 - t], 16)
            pool.wait_ge(idx_ready[0], (TILES // 2 + 1) * 16)

        @block.tensor
        def _(pe):
            def ring(s, use):
                pe.wait_ge(s_drained, s.count(use))
                return s_ps[s.ring_slot(use)]

            def await_drained(s, use):
                pe.wait_ge(s_drained, s.count(use) + NS)

            def turn(s, half):
                bank = ring(s, f"turn{half}")[:, :].bitcast(BF16)
                if half == 0:
                    for part in (part0_ready, part1_ready, part2_ready):
                        pe.wait_ge(part, s.tile(1, 2))
                for d in range(DT):
                    mm = nc.tensor.transpose(bank[0:CH, d * P:(d + 1) * P],
                                             parts[:, half * DT + d, :, :].rearrange("p a f -> p (a f)"), idb[:, :])
                mm.then_inc(s_full, 1)

            def quarter(t, q):
                return emb_t[t][:, :, :].rearrange("p b d -> p (b d)")[:, q * BANK:(q + 1) * BANK]

            def operand_a(s, q):
                if q == 0:
                    await_drained(s, "turn1")
                nc.tensor.matmul(ring(s, f"a{q}")[0:CH, :], pick_sb[:, A_AT:A_AT + CH],
                                 quarter(s.next_parity, q), start=True, stop=True).then_inc(s_full, 1)

            def unit(s, u):
                half, c = divmod(u, NCH)
                pe.wait_ge(low_ready, s.tile(UNITS, u + 1))
                if c == 0:
                    pe.wait_ge(x1_ready, s.tile(NX, half + 1))
                n = slot(s, u)
                passes = ((w0h, prod_h[n]), (w0h, prod_l[n]), (w0l, prod_h[n]))
                for k, (w, x) in enumerate(passes):
                    for q in range(2):
                        mm = nc.tensor.matmul(x1_ps[:, half * HALF + q * BANK:half * HALF + (q + 1) * BANK],
                                              w[:, c, :], x[:, q * BANK:(q + 1) * BANK],
                                              start=(c == 0 and k == 0),
                                              stop=(c == NCH - 1 and k == len(passes) - 1))
                mm.then_inc(unit_done, 1)

            def ecols(s, q):
                back = q == 3
                pe.wait_ge(ediag_ready, s.tile(QUARTERS, q + 1 - QUARTERS * back))
                if q == 0 and s.previous:
                    pe.wait_ge(z2_ready, s.tile(1, 0))
                t = 1 - s.t if back else s.t
                for g in range(GROUPS):
                    mm = nc.tensor.matmul(misc_ps[:, g * FE:(g + 1) * FE], quarter(t, q)[:, g * P:(g + 1) * P],
                                          pick_sb[:, E_AT:E_AT + FE], start=True, stop=True)
                mm.then_inc(ecol_full, 1)

            def x1_turn(s, q):
                pe.wait_ge(x1_ready, s.tile(NX, NX + 1 if q < 2 else 2))
                bank = ring(s, f"x1t{q}")
                for g in range(GROUPS):
                    at = (q * GROUPS + g) * P
                    mm = nc.tensor.transpose(bank[:, g * P:(g + 1) * P], x1[:, at:at + P], idf[:, :])
                mm.then_inc(s_full, 1)

            def interact(s, n):
                q, g = divmod(n, GROUPS)
                if g == 0:
                    await_drained(s, f"x1t{q}")
                    pe.wait_ge(ediag_ready, s.tile(QUARTERS, q + 2 - (QUARTERS if q >= 2 else 0)))
                nc.tensor.matmul(ring(s, f"g{n}")[:, 0:GRP * FE], x1t[q % 2][:, g, :],
                                 ediag[q % 2][:, g, :, :].rearrange("p b f -> p (b f)"),
                                 start=True, stop=True).then_inc(s_full, 1)

            def layer1(s, f):
                if f == 0:
                    await_drained(s, f"g{QUARTERS * GROUPS - 1}")
                    pe.wait_ge(ediag_ready, s.tile(QUARTERS, 1))
                mm = nc.tensor.matmul(misc_ps[:, 0:P], w1_sb[:, f, :], g_sb[:, f, :],
                                      start=(f == 0), stop=(f == FIELDS - 1))
                if f == FIELDS - 1:
                    mm.then_inc(z2_full, 1)

            def dense_layer(s, use, w, rows, m, outs, first=0):
                if m == 0:
                    ring(s, use)
                at = (first + m) * P
                for k, x in enumerate(rows):
                    mm = nc.tensor.matmul(s_ps[s.ring_slot(use)][:, m * P:(m + 1) * P], w[:, k, at:at + P], x,
                                          start=(k == 0), stop=(k == len(rows) - 1))
                if m == outs - 1:
                    mm.then_inc(s_full, 1)

            def beside(s, u):
                for piece, n in s.beside(u):
                    if piece == "ecols":
                        ecols(s, n)
                    elif piece == "z2":
                        layer1(s, n)
                    elif piece in ("h1a", "h1b"):
                        if (piece, n) == ("h1a", 0):
                            pe.wait_ge(z2_ready, s.tile(1, 0))
                        dense_layer(s, piece, wt1, (g_sb[:, FIELDS, :], z2[:, :],
                                                    dense_sb[:, bass.ds(s.tile(P, -P), P)]), n, MT1 // 2,
                                    MT1 // 2 * (piece == "h1b"))
                    elif piece == "h2":
                        if n == 0:
                            await_drained(s, "h1b")
                        dense_layer(s, "h2", wt2, [h1[:, k, :] for k in range(MT1)], n, MT2)
                    elif piece == "y":
                        await_drained(s, "h2")
                        dense_layer(s, "y", wt3, [h2[:, k, :] for k in range(MT2)], n, 1)
                    elif piece.startswith("x1t"):
                        x1_turn(s, int(piece[3:]))
                    elif piece.startswith("turn"):
                        turn(s, int(piece[4:]))
                    elif piece.startswith("a"):
                        operand_a(s, int(piece[1:]))
                    elif piece.startswith("g"):
                        interact(s, int(piece[1:]))

            def opening(s):
                pe.sem_inc(unit_done, NP)
                pe.wait_ge(loads, 16 * len(LOADS))
                turn(s, 0)
                turn(s, 1)
                for q in range(QUARTERS):
                    operand_a(s, q)
                pe.wait_ge(w0_ready, 1)

            def step(s):
                for u in range(UNITS):
                    if s.layer0:
                        unit(s, u)
                    beside(s, u)

            steps(pe, opening, step)

        @block.scalar
        def _(act):
            def full(s, use):
                act.wait_ge(s_full, s.count(use))
                return s_ps[s.ring_slot(use)]

            def split(s, n):
                t = s.next_parity
                if n == 0:
                    act.wait_ge(gathered[t], (s.i + (s.t + 1) // 2 + 1) * (16 * FIELDS))
                else:
                    act.wait_ge(rest_ready, s.tile(1, 2 + 2))
                nc.scalar.copy(parts[:, :, n, :], (emb[t] if n == 0 else rest)[:, :, :].rearrange("p f d -> p d f")
                               ).then_inc((part0_ready, part1_ready)[n], 1)

            def turned(s, half):
                t = s.next_parity
                bank = full(s, f"turn{half}")
                nc.scalar.copy(emb_t[t][:, :, half * DT:(half + 1) * DT].rearrange("p b d -> p d b"),
                               bank[:, :].bitcast(BF16)[0:CH, :].rearrange("p (d b) -> p d b", d=DT)
                               ).then_inc(s_drained, 1)

            def operand_a(s, q):
                t = s.next_parity
                nc.scalar.copy(opa[t][:, q * BANK:(q + 1) * BANK], full(s, f"a{q}")[0:CH, :]).then_inc(s_drained, 1)
                if q % 2:
                    act.drain().then_inc(a_ready[q // 2], 1)

            def high(s, u, tiles_on=0):
                act.wait_ge(multiplied, s.tile(UNITS, tiles_on * UNITS + u + 1 + NB))
                act.wait_ge(unit_done, s.tile(UNITS, tiles_on * UNITS + u + 1))
                n = slot(s, u, tiles_on)
                nc.scalar.copy(prod_h[n][:, :], prod[n][:, :]).then_inc(high_ready, 1)

            def x1_out(s, half):
                act.wait_ge(unit_done, s.tile(UNITS, (half + 1) * NCH + NP))
                cols = slice(half * HALF, (half + 1) * HALF)
                nc.scalar.copy(x1[:, cols], x1_ps[:, cols]).then_inc(x1_ready, 1)

            def g_out(s, n):
                nc.scalar.copy(g_sb[:, :, n * GRP:(n + 1) * GRP].rearrange("p f b -> p b f"),
                               full(s, f"g{n}")[:, 0:GRP * FE].rearrange("p (b f) -> p b f", b=GRP)
                               ).then_inc(s_drained, 1)

            def relu(s, use, dst, bias, outs, first=0):
                bank = full(s, use)
                for m in range(outs):
                    a = nc.scalar.activation(dst[:, first + m, :], bank[:, m * P:(m + 1) * P], ACT.Relu,
                                             bias=bias[:, first + m:first + m + 1])
                a.then_inc(s_drained, 1)

            def beside(s, u):
                for use, n in s.beside(u):
                    if use == "z2" and n == FIELDS - 1:
                        act.wait_ge(z2_full, s.tile(1, 0))
                        nc.scalar.copy(z2[:, :], misc_ps[:, 0:P]).then_inc(z2_ready, 1)
                    if use not in s.order or n != LAST_PIECE.get(use, 0):
                        continue
                    if use.startswith("x1t"):
                        q = int(use[3:])
                        nc.scalar.copy(x1t[q % 2][:, :, :].rearrange("p g h -> p (g h)"), full(s, use)[:, :]
                                       ).then_inc(s_drained, 1)
                    elif use.startswith("g"):
                        g_out(s, int(use[1:]))
                    elif use.startswith("turn"):
                        turned(s, int(use[4:]))
                    elif use.startswith("a"):
                        operand_a(s, int(use[1:]))
                    elif use == "h1a":
                        relu(s, use, h1, bt1, MT1 // 2)
                    elif use == "h1b":
                        relu(s, use, h1, bt1, MT1 // 2, MT1 // 2)
                    elif use == "h2":
                        relu(s, use, h2, bt2, MT2)
                    elif use == "y":
                        nc.scalar.copy(y[:, bass.ds(s.tile(P, -P), P)], full(s, use)[0:1, 0:P]).then_inc(s_drained, 1)

            def opening(s):
                act.sem_inc(s_drained, NS)
                act.sem_inc(x1_ready, NX)
                split(s, 0)
                split(s, 1)
                act.wait_ge(w0_sum, 1)
                nc.scalar.copy(w0h[:, :, :], w0s).then_inc(w0_high, 1)
                for half in range(2):
                    turned(s, half)
                for q in range(QUARTERS):
                    operand_a(s, q)
                for u in range(HIGH_LEAD):
                    high(s, u, 1)

            def step(s):
                for u in range(UNITS):
                    if s.layer0 and u + HIGH_LEAD < UNITS:
                        high(s, u + HIGH_LEAD)
                    elif s.layer0 and s.following:
                        high(s, u + HIGH_LEAD - UNITS, 1)
                    if s.following and u == s.split_at():
                        split(s, 0)
                    if s.following and u == s.split_at() + 1:
                        split(s, 1)
                    beside(s, u)
                    if s.layer0 and u % NCH == NCH - 1:
                        x1_out(s, u // NCH)

            steps(act, opening, step)

        @block.vector
        def _(dve):
            def split(s, n):
                if n == 0:
                    t = s.next_parity
                    dve.wait_ge(part0_ready, s.tile(1, 2))
                    nc.vector.tensor_tensor(rest[:, :, :], emb[t][:, :, :],
                                            parts[:, :, 0, :].rearrange("p d f -> p f d"),
                                            ALU.subtract).then_inc(rest_ready, 1)
                else:
                    dve.wait_ge(part1_ready, s.tile(1, 2))
                    nc.vector.tensor_tensor(parts[:, :, 2, :], rest[:, :, :].rearrange("p f d -> p d f"),
                                            parts[:, :, 1, :], ALU.subtract).then_inc(part2_ready, 1)

            def multiply(s, u):
                half, n = u // NCH, s.t * UNITS + u
                if s.previous or u >= NP:
                    dve.wait_ge(low_ready, s.tile(UNITS, u + 1 - NP))
                if u == NCH - NB:
                    dve.wait_ge(a_ready[1], s.tile(1, 1))
                dve.wait_ge(b_ready[n % NB], s.i * (2 * UNITS // NB * 16 * SHIFTS) + (n // NB + 1) * 16 * SHIFTS)
                nc.vector.tensor_tensor(prod[n % NP][:, :], opa[s.t][:, half * HALF:(half + 1) * HALF],
                                        opb[n % NB][:, :], ALU.mult).then_inc(multiplied, 1)

            def low(s, u, tiles_on=0):
                at = tiles_on * UNITS + u
                dve.wait_ge(unit_done, s.tile(UNITS, at + 1))
                dve.wait_ge(high_ready, s.tile(UNITS, at + 1))
                n = slot(s, u, tiles_on)
                nc.vector.tensor_tensor(prod_l[n][:, :], prod[n][:, :], prod_h[n][:, :].bitcast(F32),
                                        ALU.subtract).then_inc(low_ready, 1)

            def own_blocks(s, q, back):
                use = ("g11", "g15", "g3", "g7")[q]
                if back:
                    dve.wait_ge(s_drained, s.count_before(use) + NS)
                elif use in s.order:
                    dve.wait_ge(s_drained, s.count(use) + NS)
                dve.wait_ge(ecol_full, s.tile(QUARTERS, q + 1 - QUARTERS * back))
                shape = [P, GROUPS, GRP, FIELDS]
                cols = misc_ps[:, 0:GROUPS * FE].rearrange("p (g f) -> p g f", g=GROUPS)[:, :, 0:FIELDS]
                nc.vector.tensor_tensor(ediag[q % 2][:, :, :, 0:FIELDS], cols.unsqueeze(2).to_broadcast(shape),
                                        own[:, :].unsqueeze(1).unsqueeze(3).to_broadcast(shape),
                                        ALU.mult).then_inc(ediag_ready, 1)

            def opening(s):
                dve.sem_inc(multiplied, NB)
                dve.sem_inc(rest_ready, 2)
                dve.sem_inc(ediag_ready, 1)
                nc.vector.memset(wt1[:, KT1 - 1, :], 0.0).then_inc(pads_ready, 1)
                nc.vector.memset(dense_sb[:, :], 0.0).then_inc(pads_ready, 1)
                dve.wait_ge(loads, 16 * len(LOADS))
                nc.vector.tensor_tensor(w0s, w0_raw[0], w0_raw[1], ALU.add).then_inc(w0_sum, 1)
                for n in range(2):
                    nc.vector.tensor_copy(ediag[n][:, :, :, FIELDS],
                                          own[:, :].unsqueeze(1).to_broadcast([P, GROUPS, GRP]))
                split(s, 0)
                split(s, 1)
                dve.wait_ge(w0_high, 1)
                nc.vector.tensor_tensor(w0l[:, :, :], w0s, w0h[:, :, :].bitcast(F32),
                                        ALU.subtract).then_inc(w0_ready, 1)

            def step(s):
                for u in range(UNITS):
                    if s.layer0:
                        multiply(s, u)
                    if u:
                        if s.layer0:
                            low(s, u - 1)
                    elif s.previous:
                        low(s, UNITS - 1, -1)
                    for q in range(QUARTERS):
                        back, at = divmod(s.own_blocks_at(q), UNITS)
                        if u == at and (s.previous if back else s.layer0):
                            own_blocks(s, q, back)
                    if s.following and u == s.split_at() + HIGH_LEAD:
                        split(s, 0)
                    if s.following and u == s.split_at() + HIGH_LEAD + 1:
                        split(s, 1)

            steps(dve, opening, step)


def _constants():
    one = 0x3F80
    part_field = np.arange(CH) % FIELDS
    wanted = [np.arange(CH) % FIELDS, np.arange(FE)]
    pick = np.where(part_field[:, None] == np.concatenate(wanted)[None, :], one, 0).astype(np.uint16)
    own_rows = (np.arange(P)[:, None] // D == np.arange(GRP)[None, :]).astype(np.float32)
    return {"pick": pick, "ident_bf": np.where(np.eye(P) == 1, one, 0).astype(np.uint16),
            "ident_f": np.eye(P, dtype=np.float32), "own_rows": own_rows}


def _pair_weights(w0):
    w = w0.reshape(H, FIELDS, FIELDS)
    ij = np.zeros((CH, NCH, H), w0.dtype)
    ji = np.zeros((CH, NCH, H), w0.dtype)
    i = np.arange(FIELDS)
    for t in range(NCH):
        for k in range(SHIFTS):
            s = SHIFTS * t + k
            rows = slice(k * FIELDS, (k + 1) * FIELDS)
            j = (i + s) % FIELDS
            ij[rows, t] = w[:, i, j].T
            if 0 < s < FIELDS // 2:
                ji[rows, t] = w[:, j, i].T
    return ij, ji


def kernel(**inputs):
    import concourse.bacc as bacc
    from concourse.bass_utils import run_bass_kernel_spmd

    a = {k: np.ascontiguousarray(v) for k, v in inputs.items()}
    arrays = {"ids": np.pad(a["ids"], ((0, P), (0, 0))).reshape(TILES + 1, P, FIELDS)}
    arrays |= {f"tbl_{f}": a[f"tbl_{f}"] for f in range(FIELDS)}
    arrays["dense_t"] = np.ascontiguousarray(a["dense_ctx"].T)
    arrays["w0_ij"], arrays["w0_ji"] = _pair_weights(a["L0_rec_W0"])
    arrays["w1_t"] = np.ascontiguousarray(a["L0_rec_W1"].reshape(H, H, FIELDS).transpose(1, 2, 0))
    arrays |= {"w_top1": a["W_top1"], "w_top2": a["W_top2"], "w_top3": np.pad(a["W_top3"], ((0, 0), (0, P - 1))),
               "b_top1": np.ascontiguousarray(a["b_top1"].reshape(MT1, P).T),
               "b_top2": np.ascontiguousarray(a["b_top2"].reshape(MT2, P).T)}
    arrays |= _constants()

    nc = bacc.Bacc("TRN2", target_bir_lowering=False, num_devices=1)
    ap = {k: nc.dram_tensor(k, v.shape, mybir.dt.from_np(v.dtype), kind="ExternalInput").ap()
          for k, v in arrays.items()}
    out = nc.dram_tensor("score", (1, B), F32, kind="ExternalOutput").ap()
    tables = [ap.pop(f"tbl_{f}") for f in range(FIELDS)]
    cin_tower(nc, tables=tables, out=out, **ap)
    r = run_bass_kernel_spmd(nc, [arrays], core_ids=[0])
    return r.results[0]["score"].reshape(B, 1)
```
